# Optimizing a Trainium2 kernel written in Bass

```python
import numpy as np
import jax
import jax.numpy as jnp

def _softmax(x, axis=-1):
    return jax.nn.softmax(x, axis=axis)

def _gelu(x):
    return jax.nn.gelu(x, approximate=True)

def _silu(x):
    return jax.nn.silu(x)

def _sigmoid(x):
    return jax.nn.sigmoid(x)

def _layernorm(x, axis=-1, eps=1e-05):
    m = jnp.mean(x, axis=axis, keepdims=True)
    v = jnp.var(x, axis=axis, keepdims=True)
    return (x - m) / jnp.sqrt(v + eps)

def _scatter_add(tgt, idx, src, axis=0):
    return tgt.at[idx].add(src)

def _segment_sum(src, seg, n):
    return jax.ops.segment_sum(src, seg, n)
kernel_name = 'mk_adaln_attn_ffn_d1_seqx_r8_93ae92'

def setup_inputs(seed: int=0):
    np.random.seed(seed)
    _w = jnp.asarray

    def _rec_inputs():
        import jax
        import jax.numpy as jnp
        _rk = jax.random.key(seed)
        x = -0.0003929 + 0.9999 * jax.random.normal(jax.random.fold_in(_rk, 1), (128, 32, 128), jnp.float32)
        _lenS = 32 - jax.random.randint(jax.random.fold_in(_rk, 7), (128,), 0, max(1, 32 // 4) + 1, jnp.int32)
        _lenS2 = 32 - jax.random.randint(jax.random.fold_in(_rk, 8), (128,), 0, max(1, 32 // 4) + 1, jnp.int32)
        itok_B_0_2 = jax.random.randint(jax.random.fold_in(_rk, 11), (128,), 0, 3, jnp.int32)
        itok_B_0_63 = jax.random.randint(jax.random.fold_in(_rk, 12), (128,), 0, 64, jnp.int32)
        return (x, itok_B_0_2, itok_B_0_63)
    x, itok_B_0_2, itok_B_0_63 = _rec_inputs()

    def _L0_cond_setup():
        import jax, jax.numpy as jnp
        import numpy as np
        NEG_INF = -1e+30
        key = jax.random.key(seed)
        k1, k2, k3, k4, k5 = jax.random.split(key, 5)
        B, S, D, A = (16, 128, 128, 32)
        hidden = jax.random.normal(k1, (B, S, D), dtype=jnp.float32)
        W1 = jax.random.normal(k2, (D, A), dtype=jnp.float32) / np.sqrt(D)
        b1 = jax.random.normal(k3, (A,), dtype=jnp.float32) * 0.01
        v = jax.random.normal(k4, (A,), dtype=jnp.float32) / np.sqrt(A)
        prompt_type_ids = jax.random.randint(k5, (B,), 0, 3, dtype=jnp.int32)
        return {'hidden': hidden, 'W1': W1, 'b1': b1, 'v': v, 'prompt_type_ids': prompt_type_ids}
    _L0_cond_all = _L0_cond_setup()
    _L0_cond_in = {k: v for k, v in _L0_cond_all.items() if k in ('W1', 'b1', 'v')}
    del _L0_cond_all

    def _L0_attn_setup():
        import jax, jax.numpy as jnp
        import numpy as np
        import math
        D_MODEL, D_C, D_R, NH = (128, 128, 32, 16)
        HD = D_MODEL // NH
        B, T = (2, 256)

        def _rope_tables(T, d_R):
            inv_freq = 1.0 / 10000.0 ** (jnp.arange(0, d_R, 2, dtype=jnp.float32) / d_R)
            t = jnp.arange(T, dtype=jnp.float32)
            freqs = jnp.outer(t, inv_freq)
            return (jnp.cos(freqs), jnp.sin(freqs))

        def _rotary_apply(x, cos, sin):
            d = x.shape[-1]
            x1, x2 = (x[..., :d // 2], x[..., d // 2:])
            return jnp.concatenate([x1 * cos - x2 * sin, x2 * cos + x1 * sin], axis=-1)
        key = jax.random.key(seed)
        ks = jax.random.split(key, 8)
        s = lambda fan_in: 1.0 / math.sqrt(fan_in)
        return {'x': jax.random.normal(ks[0], (B, T, D_MODEL), jnp.float32), 'W_kv_down': jax.random.normal(ks[1], (D_MODEL, D_C), jnp.float32) * s(D_MODEL), 'W_k_up': jax.random.normal(ks[2], (D_C, D_MODEL), jnp.float32) * s(D_C), 'W_v_up': jax.random.normal(ks[3], (D_C, D_MODEL), jnp.float32) * s(D_C), 'W_q': jax.random.normal(ks[4], (D_MODEL, D_MODEL), jnp.float32) * s(D_MODEL), 'W_q_rope': jax.random.normal(ks[5], (D_MODEL, D_R), jnp.float32) * s(D_MODEL), 'W_k_rope': jax.random.normal(ks[6], (D_C, D_R), jnp.float32) * s(D_C), 'W_o': jax.random.normal(ks[7], (D_MODEL, D_MODEL), jnp.float32) * s(D_MODEL)}
    _L0_attn_all = _L0_attn_setup()
    _L0_attn_in = {k: v for k, v in _L0_attn_all.items() if k in ('W_kv_down', 'W_k_up', 'W_v_up', 'W_q', 'W_q_rope', 'W_k_rope', 'W_o')}
    del _L0_attn_all

    def _L0_cond2_setup():
        import jax, jax.numpy as jnp
        import numpy as np
        NUM_CATEGORIES = 64
        INPUT_DIM = 128
        HIDDEN_DIM = 128
        B = 32
        S = 64
        key = jax.random.key(seed)
        kx, kc, kw = jax.random.split(key, 3)
        x = jax.random.normal(kx, (B, S, INPUT_DIM), dtype=jnp.float32)
        cat_ids = jax.random.randint(kc, (B,), 0, NUM_CATEGORIES, dtype=jnp.int32)
        W = 0.02 * jax.random.normal(kw, (NUM_CATEGORIES, INPUT_DIM, HIDDEN_DIM), dtype=jnp.float32)
        b = jnp.zeros((NUM_CATEGORIES, HIDDEN_DIM), dtype=jnp.float32)
        return {'x': x, 'cat_ids': cat_ids, 'W': W, 'b': b}
    _L0_cond2_all = _L0_cond2_setup()
    _L0_cond2_in = {k: v for k, v in _L0_cond2_all.items() if k in ('W', 'b')}
    del _L0_cond2_all

    def _L0_ffn_setup():
        import jax, jax.numpy as jnp
        import numpy as np
        B, S, H = (2, 256, 128)
        E, F, K = (64, 64, 8)
        G, TG = (8, 4)
        SCALE = 2.5
        F_SH = 64

        def _gate(x, gate_w, gate_bias):
            scores = jax.nn.sigmoid(x @ gate_w.T)
            sc = scores + gate_bias[None, :]
            T = x.shape[0]
            group_scores = jax.lax.top_k(sc.reshape(T, G, E // G), 2)[0].sum(-1)
            _, gidx = jax.lax.top_k(group_scores, TG)
            gmask = jnp.zeros((T, G), sc.dtype).at[jnp.arange(T)[:, None], gidx].set(1.0)
            smask = jnp.repeat(gmask, E // G, axis=1)
            masked = jnp.where(smask > 0, sc, -jnp.inf)
            _, tidx = jax.lax.top_k(masked, K)
            tw = jnp.take_along_axis(scores, tidx, axis=1)
            tw = tw / (tw.sum(-1, keepdims=True) + 1e-20)
            return (tidx, tw * SCALE)
        key = jax.random.key(seed)
        ks = jax.random.split(key, 9)

        def w(k, shape, fan_in):
            return jax.random.normal(k, shape, jnp.float32) / np.float32(np.sqrt(fan_in))
        return {'hidden_states': jax.random.normal(ks[0], (B, S, H), jnp.float32), 'gate_w': w(ks[1], (E, H), H), 'gate_bias': jax.random.normal(ks[2], (E,), jnp.float32) * 0.01, 'We_gate': w(ks[3], (E, H, F), H), 'We_up': w(ks[4], (E, H, F), H), 'We_down': w(ks[5], (E, F, H), F), 'Ws_gate': w(ks[6], (H, F_SH), H), 'Ws_up': w(ks[7], (H, F_SH), H), 'Ws_down': w(ks[8], (F_SH, H), F_SH)}
    _L0_ffn_all = _L0_ffn_setup()
    _L0_ffn_in = {k: v for k, v in _L0_ffn_all.items() if k in ('gate_w', 'gate_bias', 'We_gate', 'We_up', 'We_down', 'Ws_gate', 'Ws_up', 'Ws_down')}
    del _L0_ffn_all
    return {'x': x, 'itok_B_0_2': itok_B_0_2, 'itok_B_0_63': itok_B_0_63, 'L0_cond_W1': _L0_cond_in['W1'], 'L0_cond_b1': _L0_cond_in['b1'], 'L0_cond_v': _L0_cond_in['v'], 'L0_attn_W_kv_down': _L0_attn_in['W_kv_down'], 'L0_attn_W_k_up': _L0_attn_in['W_k_up'], 'L0_attn_W_v_up': _L0_attn_in['W_v_up'], 'L0_attn_W_q': _L0_attn_in['W_q'], 'L0_attn_W_q_rope': _L0_attn_in['W_q_rope'], 'L0_attn_W_k_rope': _L0_attn_in['W_k_rope'], 'L0_attn_W_o': _L0_attn_in['W_o'], 'L0_cond2_W': _L0_cond2_in['W'], 'L0_cond2_b': _L0_cond2_in['b'], 'L0_ffn_gate_w': _L0_ffn_in['gate_w'], 'L0_ffn_gate_bias': _L0_ffn_in['gate_bias'], 'L0_ffn_We_gate': _L0_ffn_in['We_gate'], 'L0_ffn_We_up': _L0_ffn_in['We_up'], 'L0_ffn_We_down': _L0_ffn_in['We_down'], 'L0_ffn_Ws_gate': _L0_ffn_in['Ws_gate'], 'L0_ffn_Ws_up': _L0_ffn_in['Ws_up'], 'L0_ffn_Ws_down': _L0_ffn_in['Ws_down']}

def reference(x, itok_B_0_2, itok_B_0_63, L0_cond_W1, L0_cond_b1, L0_cond_v, L0_attn_W_kv_down, L0_attn_W_k_up, L0_attn_W_v_up, L0_attn_W_q, L0_attn_W_q_rope, L0_attn_W_k_rope, L0_attn_W_o, L0_cond2_W, L0_cond2_b, L0_ffn_gate_w, L0_ffn_gate_bias, L0_ffn_We_gate, L0_ffn_We_up, L0_ffn_We_down, L0_ffn_Ws_gate, L0_ffn_Ws_up, L0_ffn_Ws_down):
    import jax
    import jax.numpy as jnp

    def _L0_cond_ref(hidden, W1, b1, v, prompt_type_ids):
        import jax, jax.numpy as jnp
        import numpy as np
        NEG_INF = -1e+30
        B, S, D = hidden.shape
        attn_in = jnp.tanh(jnp.einsum('bsd,da->bsa', hidden, W1) + b1)
        scores = jnp.einsum('bsa,a->bs', attn_in, v)
        idx = jnp.arange(S)
        j = idx[:, None]
        l = idx[None, :]
        prefix_m = l <= j
        postfix_m = l >= j
        cloze_m = l != j
        pt = prompt_type_ids[:, None, None]
        mask = jnp.where(pt == 0, prefix_m[None], jnp.where(pt == 1, postfix_m[None], cloze_m[None]))
        masked_scores = jnp.where(mask, scores[:, None, :], NEG_INF)
        p = jax.nn.softmax(masked_scores, axis=-1)
        cnt = jnp.sum(mask, axis=-1).astype(hidden.dtype)
        pooled = jnp.einsum('bjl,bld->bjd', p, hidden) / cnt[..., None]
        return pooled

    def _L0_attn_ref(x, W_kv_down, W_k_up, W_v_up, W_q, W_q_rope, W_k_rope, W_o):
        import jax, jax.numpy as jnp
        import numpy as np
        import math
        D_MODEL, D_C, D_R, NH = (128, 128, 32, 16)
        HD = D_MODEL // NH
        B, T = (2, 256)

        def _rope_tables(T, d_R):
            inv_freq = 1.0 / 10000.0 ** (jnp.arange(0, d_R, 2, dtype=jnp.float32) / d_R)
            t = jnp.arange(T, dtype=jnp.float32)
            freqs = jnp.outer(t, inv_freq)
            return (jnp.cos(freqs), jnp.sin(freqs))

        def _rotary_apply(x, cos, sin):
            d = x.shape[-1]
            x1, x2 = (x[..., :d // 2], x[..., d // 2:])
            return jnp.concatenate([x1 * cos - x2 * sin, x2 * cos + x1 * sin], axis=-1)
        Bb, Tt, _ = x.shape
        cos, sin = _rope_tables(Tt, D_R)
        cos = cos[None]
        sin = sin[None]
        c_kv = x @ W_kv_down
        k_rope = _rotary_apply(c_kv @ W_k_rope, cos, sin)
        k = (c_kv @ W_k_up).reshape(Bb, Tt, NH, HD)
        v = (c_kv @ W_v_up).reshape(Bb, Tt, NH, HD)
        q = (x @ W_q).reshape(Bb, Tt, NH, HD)
        q_rope = _rotary_apply(x @ W_q_rope, cos, sin)
        scale = math.sqrt(HD + D_R)
        scores = jnp.einsum('bqhd,bkhd->bhqk', q, k)
        scores = scores + jnp.einsum('bqr,bkr->bqk', q_rope, k_rope)[:, None]
        scores = scores / scale
        causal = jnp.triu(jnp.ones((Tt, Tt), dtype=bool), k=1)
        scores = jnp.where(causal[None, None], -jnp.inf, scores)
        w = jax.nn.softmax(scores, axis=-1)
        attn = jnp.einsum('bhqk,bkhd->bqhd', w, v).reshape(Bb, Tt, D_MODEL)
        return attn @ W_o

    def _L0_cond2_ref(x, cat_ids, W, b):
        import jax, jax.numpy as jnp
        import numpy as np
        NUM_CATEGORIES = 64
        INPUT_DIM = 128
        HIDDEN_DIM = 128
        B = 32
        S = 64
        selected_W = W[cat_ids]
        selected_b = b[cat_ids]
        out = jnp.einsum('bsd,bdh->bsh', x, selected_W) + selected_b[:, None, :]
        return out

    def _L0_ffn_ref(hidden_states, gate_w, gate_bias, We_gate, We_up, We_down, Ws_gate, Ws_up, Ws_down):
        import jax, jax.numpy as jnp
        import numpy as np
        B, S, H = (2, 256, 128)
        E, F, K = (64, 64, 8)
        G, TG = (8, 4)
        SCALE = 2.5
        F_SH = 64

        def _gate(x, gate_w, gate_bias):
            scores = jax.nn.sigmoid(x @ gate_w.T)
            sc = scores + gate_bias[None, :]
            T = x.shape[0]
            group_scores = jax.lax.top_k(sc.reshape(T, G, E // G), 2)[0].sum(-1)
            _, gidx = jax.lax.top_k(group_scores, TG)
            gmask = jnp.zeros((T, G), sc.dtype).at[jnp.arange(T)[:, None], gidx].set(1.0)
            smask = jnp.repeat(gmask, E // G, axis=1)
            masked = jnp.where(smask > 0, sc, -jnp.inf)
            _, tidx = jax.lax.top_k(masked, K)
            tw = jnp.take_along_axis(scores, tidx, axis=1)
            tw = tw / (tw.sum(-1, keepdims=True) + 1e-20)
            return (tidx, tw * SCALE)
        b, s, h = hidden_states.shape
        x = hidden_states.reshape(-1, h).astype(jnp.float32)
        tidx, tw = _gate(x, gate_w, gate_bias)
        T = x.shape[0]
        w_dense = jnp.zeros((T, E), tw.dtype).at[jnp.arange(T)[:, None], tidx].add(tw)

        def body(acc, ws):
            wg, wu, wdn, cw = ws
            hmid = jax.nn.silu(x @ wg) * (x @ wu)
            return (acc + cw[:, None] * (hmid @ wdn), None)
        y, _ = jax.lax.scan(body, jnp.zeros_like(x), (We_gate, We_up, We_down, w_dense.T))
        y = y.reshape(b, s, h)
        shared = jax.nn.silu(hidden_states @ Ws_gate) * (hidden_states @ Ws_up) @ Ws_down
        return y + shared
    x = x + _L0_attn_ref(_L0_cond_ref(x, L0_cond_W1, L0_cond_b1, L0_cond_v, itok_B_0_2), L0_attn_W_kv_down, L0_attn_W_k_up, L0_attn_W_v_up, L0_attn_W_q, L0_attn_W_q_rope, L0_attn_W_k_rope, L0_attn_W_o)
    x = x + _L0_ffn_ref(_L0_cond2_ref(x, itok_B_0_63, L0_cond2_W, L0_cond2_b), L0_ffn_gate_w, L0_ffn_gate_bias, L0_ffn_We_gate, L0_ffn_We_up, L0_ffn_We_down, L0_ffn_Ws_gate, L0_ffn_Ws_up, L0_ffn_Ws_down)
    return x

_drawn_inputs = setup_inputs


def setup_inputs(seed=0):
    import zlib

    import numpy as np

    out = dict(_drawn_inputs(seed))
    spreads = {'L0_cond2_b': (0.0, 0.273)}
    factors = {'L0_cond_b1': 185.245,
     'L0_attn_W_k_up': 8.0,
     'L0_attn_W_q': 8.0,
     'L0_attn_W_q_rope': 5.4,
     'L0_attn_W_k_rope': 5.476,
     'L0_ffn_gate_bias': 4.898}
    for name, (base, spread) in spreads.items():
        noise = np.random.default_rng([zlib.crc32(name.encode()), seed]).standard_normal(out[name].shape)
        drawn = base * np.exp(spread * noise) if base else spread * noise
        out[name] = jnp.asarray(drawn.astype(out[name].dtype))
    for name, factor in factors.items():
        out[name] = (out[name] * factor).astype(out[name].dtype)
    return out
```

```python
import numpy as np
import concourse.bass as bass
from concourse import mybir
from concourse.alu_op_type import AluOpType as ALU
from contextlib import ExitStack

F32 = mybir.dt.float32
F32R = mybir.dt.float32r
I32 = mybir.dt.int32
ACT = mybir.ActivationFunctionType
AX = mybir.AxisListType.X

P = 128
D = 128
SEQ = 32
NSEQ = 128
HEADS, HD = 16, 8
ROPE = 32
TOK = 512
NBLK = NSEQ * SEQ // TOK
TILES = TOK // P
SPT = P // SEQ
SPB = TOK // SEQ
CATS = 64
E, F = 64, 64
GROUPS, PER_GROUP, TOP_GROUPS, TOP_K = 8, 8, 4, 8
ROUTE_SCALE = 2.5
NPAIR = E // 2
UNITS = NPAIR + 1
ATT_SCALE = 1.0 / float(np.sqrt(HD + ROPE))
MASKED = -1.0e30
HG = 4
NG = HEADS // HG
VC = HD + 1

W_COLS, W_TOTAL = {}, 0
for _n, _w in (("kv", D), ("q", D), ("k", D), ("v", D), ("o", D), ("qr", 2 * ROPE), ("kr", 2 * ROPE),
               ("w1", 32), ("gate", E)):
    W_COLS[_n] = (W_TOTAL, _w)
    W_TOTAL += _w
C_COLS, C_TOTAL = {}, 0
for _n, _w in (("ident", P), ("head_of_group", HG), ("group", NG), ("causal", SEQ), ("neg0", SEQ), ("neg1", SEQ),
               ("neg2", SEQ), ("count", 3), ("cos", SEQ), ("sin", SEQ), ("lower", GROUPS * GROUPS), ("index", 1)):
    C_COLS[_n] = (C_TOTAL, _w)
    C_TOTAL += _w


def shape_constants():
    c = np.zeros((P, C_TOTAL), np.float32)

    def col(name):
        a, w = C_COLS[name]
        return c[:, a:a + w]

    p = np.arange(P)
    j = (p % SEQ)[:, None]
    l = np.arange(SEQ)[None, :]
    col("ident")[:] = np.eye(P)
    col("head_of_group")[:] = (p % 32 // HD)[:, None] == np.arange(HG)
    col("group")[:] = (p // 32)[:, None] == np.arange(NG)
    col("causal")[:] = np.where(l <= j, 0.0, MASKED)
    for name, seen in (("neg0", l <= j), ("neg1", l >= j), ("neg2", l != j)):
        col(name)[:] = np.where(seen, 0.0, MASKED)
        col("count")[:, int(name[-1])] = seen.sum(1)
    inv = (1.0 / np.float32(10000.0) ** (np.arange(0, ROPE, 2, dtype=np.float32) / ROPE)).astype(np.float32)
    angle = np.outer(inv, np.arange(SEQ, dtype=np.float32)).astype(np.float32)
    half = p % ROPE % (ROPE // 2)
    col("cos")[:] = np.cos(angle)[half]
    col("sin")[:] = np.sin(angle)[half] * np.where(p % ROPE < ROPE // 2, -1.0, 1.0)[:, None]
    g = np.arange(GROUPS)
    col("lower")[:] = (g[None, :] < g[:, None]).reshape(1, -1)
    col("index")[:, 0] = p
    return c


def adaln_attention_moe(nc, x_tok, x_feat, prompt, cats, cond_w, cond_b, weights, consts, b1v, gate_bias,
                        we_gate, we_up, we_down, ws_gu, ws_down, out):
    ctx = ExitStack()
    with ctx:
        def sb(name, shape, dt=F32):
            return ctx.enter_context(nc.sbuf_tensor(name, shape, dt))

        def sem(name):
            return ctx.enter_context(nc.semaphore(name))

        w = sb("w", [P, W_TOTAL])
        c = sb("c", [P, C_TOTAL])
        W = {n: w[:, a:a + k] for n, (a, k) in W_COLS.items()}
        C = {n: c[:, a:a + k] for n, (a, k) in C_COLS.items()}
        wg_hi, wg_lo = sb("wg_hi", [P, UNITS, P], F32R), sb("wg_lo", [P, UNITS, P], F32R)
        wu_hi, wu_lo = sb("wu_hi", [P, UNITS, P], F32R), sb("wu_lo", [P, UNITS, P], F32R)
        wd_hi, wd_lo = sb("wd_hi", [P, UNITS, D], F32R), sb("wd_lo", [P, UNITS, D], F32R)
        bv = sb("bv", [32, 2])
        vrep = sb("vrep", [32, P])
        gbias = sb("gbias", [P, E])
        cat_bias = sb("cat_bias", [CATS, D])
        cat_row = sb("cat_row", [CATS, NSEQ], I32)
        onehot = sb("onehot", [CATS, NSEQ])
        pt_i = sb("pt_i", [P, NSEQ // SPT], I32)
        pt_f = sb("pt_f", [P, 4, NSEQ // SPT])
        neg = sb("neg", [P, NSEQ // SPT, SEQ])
        cnt = sb("cnt", [P, 2, NSEQ // SPT])

        xt = sb("xt", [P, TILES, D])
        xf = sb("xf", [P, TOK])
        s_t = sb("s_t", [P, TILES, HEADS * SEQ])
        th = s_t[0:32, 0, :]
        pool_p = s_t[:, 1, 0:TILES * SEQ].rearrange("p (t l) -> p t l", l=SEQ)
        pool_pt = sb("pool_pt", [P, TILES, SPT, SEQ])
        small = sb("small", [P, 16])
        h_feat = sb("h_feat", [P, TOK])
        ckv = sb("ckv", [P, TOK])
        q_grp = sb("q_grp", [P, NG, TOK])
        k_blk = sb("k_blk", [P, HG, TOK])
        wcat = k_blk[:, :, :].rearrange("p a b -> p (a b)").rearrange("p (s h) -> p s h", h=D)
        v_blk = sb("v_blk", [P, TILES, SPT, NG, HG * VC])
        pt_sb = sb("pt_sb", [P, 2, NG * P])
        rot = pt_sb[0:2 * ROPE]
        qk_rope = sb("qk_rope", [ROPE, 2, TOK])
        rope_mask = sb("rope_mask", [P, TILES, SEQ])
        head_max = sb("head_max", [P, TILES, HEADS])
        rden = sb("rden", [P, TILES, HEADS])
        att = ckv[:, :].rearrange("p (t h d) -> p t h d", t=TILES, h=HEADS)
        att_feat = h_feat
        x2_next = sb("x2_next", [P, TOK])
        c2 = sb("c2", [P, TOK])
        score = sb("score", [P, TILES, E])
        biased = sb("biased", [P, TILES, E])
        rt = sb("rt", [P, 3, TILES * E])
        best = sb("best", [P, TILES, 8])
        cw = sb("cw", [P, TILES, E])
        cw_feat = sb("cw_feat", [2 * E, TOK // 2])
        cat_reg = cat_row[0:1, :]

        c_hi, c_lo = sb("c_hi", [P, TOK], F32R), sb("c_lo", [P, TOK], F32R)
        x2 = sb("x2", [P, TOK])
        NCW = 4
        cwb = sb("cwb", [P, NCW, TOK])
        act_w = sb("act_w", [P, 2, TOK])
        hid = sb("hid", [P, 2, TOK])
        hid_hi, hid_lo = sb("hid_hi", [P, 2, TOK], F32R), sb("hid_lo", [P, 2, TOK], F32R)
        y = sb("y", [P, TOK])
        stage = cwb

        cw_dram = nc.dram_tensor("cw_scratch", [E, NSEQ * SEQ], F32).ap()

        def bank(name):
            return ctx.enter_context(nc.psum_tensor(name, [P, 512], F32))

        A0, A1, A2 = bank("A0"), bank("A1"), bank("A2")
        G = [bank("G0"), bank("G1")]
        U = [bank("U0"), bank("U1")]
        Y = bank("Y")

        S = {}
        for name in """consts_in small_in stage_in0 stage_in1 stage_in2 stage_in3 split_hi split_lo setup pe_x
                xt_in xf_in wcat_in cw_stored y_free cwb_in0 cwb_in1 cwb_in2 cwb_in3
                hidden_ps tanh_done score_ps pool_sub pool_exp pool_prob pooled_ps h_ready ckv_ps q_ps ckv_ready q_ready
                rope_ps rope_ready k_ps k_ready v_ps v_ready rope_score_ps rope_mask_ready score_tile_ps biased_tile
                sub_tile prob_tile probT_ps probT_ready av_ps att_ready attT_ps attT_ready wo_ps x2_ready c2_ps c2_ready
                gate_ps tanh_gate cw_ready cwT_ps cwT_ready dve_chain
                c_hi_ready c_lo_ready x2_moved gate_done silu_done up_done weighted hid_ready hi_ready lo_ready
                down_done y_ready sum_free""".split():
            S[name] = sem(name)
        stage_in = [S[f"stage_in{i}"] for i in range(4)]
        cwb_in = [S[f"cwb_in{i}"] for i in range(4)]

        def wait(eng, name, value):
            if not (isinstance(value, int) and value <= 0):
                eng.wait_ge(S[name], value)

        NSPLIT = 24
        CHAIN_SETUP = 15
        CHAIN = 40
        block = ctx.enter_context(nc.Block())

        @block.sync
        def _(sp):
            sp.dma_start(w[:, :], weights).then_inc(S["consts_in"], 16)
            sp.dma_start(c[:, :], consts).then_inc(S["consts_in"], 16)
            for dst, src in ((bv[:, :], b1v), (gbias[:, :], gate_bias.to_broadcast([P, E])), (cat_bias[:, :], cond_b),
                             (cat_row[:, :], cats.to_broadcast([CATS, NSEQ])), (pt_i[:, :], prompt)):
                sp.dma_start(dst, src).then_inc(S["consts_in"], 16)

            def attention_loads(p, blk):
                if p == 0:
                    wait(sp, "pooled_ps", blk)
                    sp.dma_start(xt[:, :, :], x_tok[:, bass.ds(blk * TILES, TILES), :]).then_inc(S["xt_in"], 16)
                    wait(sp, "x2_ready", blk)
                    sp.dma_start(xf[:, :], x_feat[:, bass.ds(blk * TOK, TOK)]).then_inc(S["xf_in"], 16)
                if 18 <= p < 26:
                    for s in range(2 * (p - 18), 2 * (p - 18) + 2):
                        cat = sp.value_load(cat_reg[0:1, bass.ds(blk * SPB + s, 1)], min_val=0, max_val=CATS - 1)
                        if s == 0:
                            sp.wait_ge(S["score_tile_ps"], blk * TILES + TILES)
                        sp.dma_start(wcat[:, s, :], cond_w[bass.ds(cat * D, D), :]).then_inc(S["wcat_in"], 16)
                if p == 32:
                    sp.wait_ge(S["cwT_ready"], blk + 1)
                    dst = cw_dram[:, bass.ds(blk * TOK, TOK)].rearrange("e (u two n) -> e u two n", two=2, n=P)
                    for i in range(2):
                        sp.dma_start(dst[:, :, i, :], cw_feat[E * i:E * i + E, :].rearrange("e (u n) -> e u n", n=P))\
                            .then_inc(S["cw_stored"], 16)

            def cwb_load(p, b):
                src = cw_dram[2 * p:2 * p + 2, bass.ds(b * TOK, TOK)].unsqueeze(1).to_broadcast([2, F, TOK])
                sp.dma_start(cwb[:, p % NCW, :], src).then_inc(cwb_in[p % NCW], 16)

            sp.wait_ge(S["consts_in"], 16 * 7)
            for p in range(UNITS):
                if p < NSPLIT:
                    if p >= 4:
                        sp.wait_ge(S["split_lo"], p - 3)
                    src = (we_gate, we_up, we_down)[p // 8][:, bass.ts(p % 8, TOK)]
                    sp.dma_start(stage[:, p % 4, :], src).then_inc(stage_in[p % 4], 16)
                elif p == NSPLIT:
                    sp.wait_ge(S["split_lo"], p - 3)
                    sp.dma_start(stage[:, 0, 0:2 * F], ws_gu).then_inc(stage_in[0], 16)
                    sp.dma_start(stage[0:F, 0, 2 * F:2 * F + D], ws_down).then_inc(S["small_in"], 16)
                attention_loads(p, 0)

            def experts_loads(b, following):
                for p in range(UNITS):
                    if p < NPAIR:
                        sp.wait_ge(S["weighted"], (b + 1) * NPAIR + max(0, p - NCW + 1))
                        if p == 0:
                            sp.wait_ge(S["cw_stored"], (b + 1) * 32)
                        cwb_load(p, b)
                    if following is not None:
                        attention_loads(p, following)

            sp.wait_ge(S["split_lo"], NSPLIT + 1)
            with sp.Fori(0, NBLK - 1) as b:
                experts_loads(b, b + 1)
            experts_loads(NBLK - 1, None)
            sp.wait_ge(S["y_free"], 16 * NBLK + 16)

        @block.scalar
        def _(act):
            def attention_step(p, blk):
                if p == 0:
                    act.wait_ge(S["hidden_ps"], blk + 1)
                    nc.scalar.activation(th, A0[0:32, :], ACT.Tanh, bias=bv[:, 0:1]).then_inc(S["tanh_done"], 1)
                elif p == 4:
                    act.wait_ge(S["pool_sub"], blk + 1)
                    nc.scalar.activation(pool_p, pool_p, ACT.Exp).then_inc(S["pool_exp"], 1)
                elif p == 7:
                    act.wait_ge(S["pooled_ps"], blk + 1)
                    nc.scalar.copy(h_feat[:, :], A0[:, :]).then_inc(S["h_ready"], 1)
                elif p == 9:
                    act.wait_ge(S["ckv_ps"], blk + 1)
                    nc.scalar.copy(ckv[:, :], A1[:, :]).then_inc(S["ckv_ready"], 1)
                    act.wait_ge(S["q_ps"], blk + 1)
                    for g in range(NG):
                        last = nc.scalar.mul(q_grp[:, g, :], A2[:, :], C["group"][:, g:g + 1])
                    last.then_inc(S["q_ready"], 1)
                elif p == 11:
                    act.wait_ge(S["k_ps"], blk + 1)
                    for h in range(HG):
                        last = nc.scalar.mul(k_blk[:, h, :], A2[:, :], C["head_of_group"][:, h:h + 1])
                    last.then_inc(S["k_ready"], 1)
                elif p == 18:
                    for t in range(TILES):
                        act.wait_ge(S["sub_tile"], blk * TILES + t + 1)
                        nc.scalar.activation(s_t[:, t, :], s_t[:, t, :], ACT.Exp, scale=ATT_SCALE)\
                            .then_inc(S["prob_tile"], 1)
                elif 19 <= p < 23:
                    t = p - 19
                    act.wait_ge(S["probT_ps"], blk * TILES + t + 1)
                    if t >= 2:
                        act.wait_ge(S["av_ps"], blk * TILES + t - 1)
                    nc.scalar.copy(pt_sb[:, t % 2, :], A1[:, :]).then_inc(S["probT_ready"], 1)
                elif p == 24:
                    act.wait_ge(S["attT_ps"], blk + 1)
                    nc.scalar.copy(att_feat[:, :], A1[:, :]).then_inc(S["attT_ready"], 1)
                elif p == 26:
                    act.wait_ge(S["c2_ps"], blk + 1)
                    nc.scalar.copy(c2[:, :], A1[:, :]).then_inc(S["c2_ready"], 1)
                elif p == 27:
                    act.wait_ge(S["gate_ps"], blk + 1)
                    nc.scalar.activation(score[:, :, :].rearrange("p t e -> p (t e)"), A2[:, 0:TILES * E], ACT.Tanh,
                                         scale=0.5).then_inc(S["tanh_gate"], 1)
                elif p == 32:
                    act.wait_ge(S["cwT_ps"], blk + 1)
                    wait(act, "cw_stored", blk * 32)
                    nc.scalar.copy(cw_feat[:, :], A0[:, 0:TOK // 2]).then_inc(S["cwT_ready"], 1)

            def switch(blk):
                wait(act, "up_done", blk * UNITS)
                act.wait_ge(S["c2_ready"], blk + 1)
                nc.scalar.copy(c_hi[:, :], c2[:, :]).then_inc(S["c_hi_ready"], 1)

            act.sem_inc(S["y_free"], 16)
            act.wait_ge(S["consts_in"], 16 * 7)
            for p in range(UNITS):
                if p < NSPLIT:
                    act.wait_ge(stage_in[p % 4], 16 * (p // 4 + 1))
                    hi = (wg_hi, wu_hi, wd_hi)[p // 8]
                    nc.scalar.copy(hi[:, 4 * (p % 8):4 * (p % 8) + 4, :].rearrange("p a b -> p (a b)"),
                                   stage[:, p % 4, :]).then_inc(S["split_hi"], 1)
                elif p == NSPLIT:
                    act.wait_ge(stage_in[0], 16 * (NSPLIT // 4 + 1))
                    act.wait_ge(S["small_in"], 16)
                    nc.scalar.copy(wg_hi[:, NPAIR, 0:F], stage[:, 0, 0:F])
                    nc.scalar.copy(wu_hi[:, NPAIR, 0:F], stage[:, 0, F:2 * F])
                    nc.scalar.copy(wd_hi[0:F, NPAIR, :], stage[0:F, 0, 2 * F:2 * F + D]).then_inc(S["split_hi"], 1)
                attention_step(p, 0)
            switch(0)

            def experts(b, following):
                def rounded(p):
                    act.wait_ge(S["hid_ready"], b * UNITS + p + 1)
                    if p >= 2:
                        act.wait_ge(S["down_done"], b * UNITS + p - 1)
                    n = P if p < NPAIR else F
                    nc.scalar.copy(hid_hi[0:n, p % 2, :], hid[0:n, p % 2, :]).then_inc(S["hi_ready"], 1)

                for p in range(UNITS):
                    act.wait_ge(S["gate_done"], b * UNITS + p + 1)
                    if p < NPAIR:
                        nc.scalar.activation(G[p % 2][:, :], G[p % 2][:, :], ACT.Silu).then_inc(S["silu_done"], 1)
                    else:
                        act.wait_ge(S["hid_ready"], b * UNITS + p - 1)
                        nc.scalar.activation(act_w[0:F, p % 2, :], G[p % 2][0:F, :], ACT.Silu)\
                            .then_inc(S["silu_done"], 1)
                    if p >= 1:
                        rounded(p - 1)
                    if following is not None:
                        attention_step(p, following)
                rounded(UNITS - 1)
                if following is not None:
                    switch(following)
                act.wait_ge(S["y_ready"], b + 1)
                act.dma_start(out[:, bass.ds(b * TOK, TOK)], y[:, :]).then_inc(S["y_free"], 16)

            with act.Fori(0, NBLK - 1) as b:
                experts(b, b + 1)
            experts(NBLK - 1, None)

        @block.gpsimd
        def _(pool):
            def attention_step(p, blk):
                if 14 <= p < 18:
                    t = p - 14
                    pool.wait_ge(S["biased_tile"], blk * TILES + t + 1)
                    s = s_t[:, t, :].rearrange("p (h k) -> p h k", k=SEQ)
                    nc.gpsimd.tensor_sub(s, s, head_max[:, t, :].unsqueeze(2).to_broadcast([P, HEADS, SEQ]))\
                        .then_inc(S["sub_tile"], 1)

            def switch(blk):
                wait(pool, "up_done", blk * UNITS)
                pool.wait_ge(S["c_hi_ready"], blk + 1)
                nc.gpsimd.tensor_sub(c_lo[:, :], c2[:, :], c_hi[:, :].bitcast(F32)).then_inc(S["c_lo_ready"], 1)

            pool.memset(pool_pt[:, :, :, :], 0.0)
            nc.gpsimd.memset(v_blk[:, :, :, :, :], 0.0).then_inc(S["setup"], 1)
            pool.wait_ge(S["setup"], 1)
            v_ones = v_blk[:, :, :, :, :].rearrange("p t s c m -> p (t s c) m")
            for r in range(HG):
                last = nc.gpsimd.memset(v_ones[32 * r:32 * r + 32, :, r * VC + HD:r * VC + VC], 1.0)
            last.then_inc(S["setup"], 1)
            pool.wait_ge(S["setup"], 2)
            for p in range(UNITS):
                if p <= NSPLIT:
                    pool.wait_ge(S["split_hi"], p + 1)
                if p < NSPLIT:
                    hi, lo = ((wg_hi, wg_lo), (wu_hi, wu_lo), (wd_hi, wd_lo))[p // 8]
                    hi, lo = (a[:, 4 * (p % 8):4 * (p % 8) + 4, :].rearrange("p a b -> p (a b)") for a in (hi, lo))
                    nc.gpsimd.tensor_sub(lo, stage[:, p % 4, :], hi.bitcast(F32)).then_inc(S["split_lo"], 1)
                elif p == NSPLIT:
                    nc.gpsimd.tensor_sub(wg_lo[:, NPAIR, 0:F], stage[:, 0, 0:F], wg_hi[:, NPAIR, 0:F].bitcast(F32))
                    nc.gpsimd.tensor_sub(wu_lo[:, NPAIR, 0:F], stage[:, 0, F:2 * F], wu_hi[:, NPAIR, 0:F].bitcast(F32))
                    nc.gpsimd.tensor_sub(wd_lo[0:F, NPAIR, :], stage[0:F, 0, 2 * F:2 * F + D],
                                         wd_hi[0:F, NPAIR, :].bitcast(F32)).then_inc(S["split_lo"], 1)
                attention_step(p, 0)
            switch(0)

            def experts(b, following):
                for p in range(UNITS):
                    pool.wait_ge(S["hi_ready"], b * UNITS + p + 1)
                    if p >= 2:
                        pool.wait_ge(S["down_done"], b * UNITS + p - 1)
                    n = P if p < NPAIR else F
                    nc.gpsimd.tensor_sub(hid_lo[0:n, p % 2, :], hid[0:n, p % 2, :],
                                         hid_hi[0:n, p % 2, :].bitcast(F32)).then_inc(S["lo_ready"], 1)
                    if following is not None:
                        attention_step(p, following)
                if following is not None:
                    switch(following)

            with pool.Fori(0, NBLK - 1) as b:
                experts(b, b + 1)
            experts(NBLK - 1, None)

        @block.vector
        def _(dve):
            steps = [0]

            def chain(ins, blk):
                steps[0] += 1
                ins.then_inc(S["dve_chain"], 1)
                dve.wait_ge(S["dve_chain"], CHAIN_SETUP + blk * CHAIN + steps[0])

            def attention_step(p, blk):
                if p == 0:
                    steps[0] = 0
                if p == 3:
                    dve.wait_ge(S["score_ps"], blk + 1)
                    for s in range(SPT):
                        q = slice(32 * s, 32 * s + 32)
                        sc = A1[q, :].rearrange("p (t s l) -> p t s l", t=TILES, s=SPT)[:, :, s, :]
                        last = nc.vector.tensor_add(pool_p[q], sc, neg[q, bass.ds(blk * TILES, TILES), :])
                    chain(last, blk)
                    chain(nc.vector.tensor_reduce(small[:, 0:TILES], pool_p, AX, ALU.max), blk)
                    nc.vector.tensor_sub(pool_p, pool_p, small[:, 0:TILES].unsqueeze(2).to_broadcast([P, TILES, SEQ]))\
                        .then_inc(S["pool_sub"], 1)
                elif p == 5:
                    dve.wait_ge(S["pool_exp"], blk + 1)
                    chain(nc.vector.tensor_reduce(small[:, 4:4 + TILES], pool_p, AX, ALU.add), blk)
                    chain(nc.vector.tensor_mul(small[:, 4:4 + TILES], small[:, 4:4 + TILES],
                                               cnt[:, 0, bass.ds(blk * TILES, TILES)]), blk)
                    chain(nc.vector.reciprocal(small[:, 8:8 + TILES], small[:, 4:4 + TILES]), blk)
                    chain(nc.vector.tensor_mul(pool_p, pool_p,
                                               small[:, 8:8 + TILES].unsqueeze(2).to_broadcast([P, TILES, SEQ])), blk)
                    for s in range(SPT):
                        q = slice(32 * s, 32 * s + 32)
                        last = nc.vector.transpose(pool_pt[q, :, s, :], pool_p[q])
                    last.then_inc(S["pool_prob"], 1)
                elif p == 10:
                    dve.wait_ge(S["rope_ps"], blk + 1)
                    for i, (ps, table) in enumerate(((A0, "cos"), (A1, "sin"))):
                        ins = nc.vector.tensor_mul(
                            rot[:, i, :].rearrange("p (s t) -> p s t", t=SEQ),
                            ps[0:2 * ROPE, :].rearrange("p (s t) -> p s t", t=SEQ),
                            C[table][0:2 * ROPE].unsqueeze(1).to_broadcast([2 * ROPE, SPB, SEQ]))
                    chain(ins, blk)
                    nc.vector.tensor_add(qk_rope[:, 0, :], rot[0:ROPE, 0, :], rot[0:ROPE, 1, :])
                    nc.vector.tensor_add(qk_rope[:, 1, :], rot[ROPE:2 * ROPE, 0, :], rot[ROPE:2 * ROPE, 1, :])\
                        .then_inc(S["rope_ready"], 1)
                elif p == 12:
                    dve.wait_ge(S["v_ps"], blk + 1)
                    for s in range(SPT):
                        for r in range(HG):
                            src = A0[32 * s:32 * s + 32, :].rearrange("p (t c r d) -> p t c r d", t=TILES, c=NG, r=HG)
                            dst = v_blk[32 * r:32 * r + 32, :, s, :, r * VC:r * VC + HD]
                            last = nc.vector.tensor_copy(dst, src[:, :, :, r, :])
                    last.then_inc(S["v_ready"], 1)
                elif p == 13:
                    dve.wait_ge(S["rope_score_ps"], blk + 1)
                    chain(nc.vector.tensor_add(rope_mask[:, :, :],
                                               A1[:, 0:TILES * SEQ].rearrange("p (t k) -> p t k", k=SEQ),
                                               C["causal"].unsqueeze(1).to_broadcast([P, TILES, SEQ])), blk)
                    dve.sem_inc(S["rope_mask_ready"], 1)
                elif 14 <= p < 18:
                    t = p - 14
                    ps = (A2, A0)[t % 2]
                    dve.wait_ge(S["score_tile_ps"], blk * TILES + t + 1)
                    s = s_t[:, t, :].rearrange("p (h k) -> p h k", k=SEQ)
                    chain(nc.vector.tensor_add(s, ps[:, :].rearrange("p (h k) -> p h k", k=SEQ),
                                               rope_mask[:, t, :].unsqueeze(1).to_broadcast([P, HEADS, SEQ])), blk)
                    nc.vector.tensor_reduce(head_max[:, t, :], s, AX, ALU.max).then_inc(S["biased_tile"], 1)
                elif 20 <= p < 24:
                    t = p - 20
                    ps = (A0, A2)[t % 2][:, 0:HEADS * VC].rearrange("p (h m) -> p h m", m=VC)
                    dve.wait_ge(S["av_ps"], blk * TILES + t + 1)
                    chain(nc.vector.reciprocal(rden[:, t, :], ps[:, :, HD]), blk)
                    nc.vector.tensor_mul(att[:, t, :, :], ps[:, :, 0:HD],
                                         rden[:, t, :].unsqueeze(2).to_broadcast([P, HEADS, HD])).then_inc(S["att_ready"], 1)
                elif p == 25:
                    dve.wait_ge(S["wo_ps"], blk + 1)
                    nc.vector.tensor_add(x2_next[:, :], A0[:, :], xf[:, :]).then_inc(S["x2_ready"], 1)
                elif p == 28:
                    routing_groups(blk)
                elif p == 29:
                    routing_experts(blk)
                elif p == 30:
                    for t in range(TILES):
                        last = nc.vector.max(best[:, t, :], biased[:, t, :])
                    chain(last, blk)
                elif p == 31:
                    routing_weights(blk)
                    assert steps[0] == CHAIN, steps[0]

            flat = biased[:, :, :].rearrange("p t (g e) -> p (t g) e", e=PER_GROUP)
            TG = TILES * GROUPS

            def scratch(i, a, n, width):
                return rt[:, i, a:a + n * width].rearrange("p (n w) -> p n w", w=width)

            def routing_groups(blk):
                dve.wait_ge(S["tanh_gate"], blk + 1)
                chain(nc.vector.tensor_scalar(score[:, :, :], score[:, :, :], 0.5, 0.5, ALU.mult, ALU.add), blk)
                chain(nc.vector.tensor_add(biased[:, :, :], score[:, :, :],
                                           gbias[:, :].unsqueeze(1).to_broadcast([P, TILES, E])), blk)
                v, width, low, at = flat, PER_GROUP // 2, None, 0
                while width:
                    a, b = v[:, :, 0:width], v[:, :, width:2 * width]
                    hi_o = scratch(0, at, TG, width)
                    lo_o = scratch(1, at, TG, width)
                    nc.vector.tensor_tensor(hi_o, a, b, ALU.max)
                    chain(nc.vector.tensor_tensor(lo_o, a, b, ALU.min), blk)
                    if low is not None:
                        other = scratch(2, 0, TG, width)
                        chain(nc.vector.tensor_tensor(other, low[:, :, 0:width], low[:, :, width:2 * width], ALU.max), blk)
                        chain(nc.vector.tensor_tensor(lo_o, lo_o, other, ALU.max), blk)
                    v, low = hi_o, lo_o
                    at += TG * width
                    width //= 2
                chain(nc.vector.tensor_add(best[:, :, :].rearrange("p t g -> p (t g)"), v[:, :, 0], low[:, :, 0]), blk)

            def routing_experts(blk):
                wide = [P, TILES, GROUPS, GROUPS]
                mine, others = best[:, :, :].unsqueeze(3).to_broadcast(wide), best[:, :, :].unsqueeze(2).to_broadcast(wide)
                above, ties = (rt[:, i, :].rearrange("p (t g o) -> p t g o", g=GROUPS, o=GROUPS) for i in (0, 1))
                nc.vector.tensor_tensor(above, others, mine, ALU.is_gt)
                chain(nc.vector.tensor_tensor(ties, others, mine, ALU.is_equal), blk)
                lower = C["lower"].unsqueeze(1).to_broadcast([P, TILES, GROUPS * GROUPS])
                tie_rows = rt[:, 1, :].rearrange("p (t n) -> p t n", n=GROUPS * GROUPS)
                chain(nc.vector.tensor_mul(tie_rows, tie_rows, lower), blk)
                chain(nc.vector.tensor_add(rt[:, 0, :], rt[:, 0, :], rt[:, 1, :]), blk)
                rank = rt[:, 2, 0:TG]
                chain(nc.vector.tensor_reduce(rank, rt[:, 0, :].rearrange("p (n o) -> p n o", o=GROUPS), AX, ALU.add), blk)
                chain(nc.vector.tensor_scalar(rank, rank, float(TOP_GROUPS), MASKED, ALU.is_ge, ALU.mult), blk)
                chain(nc.vector.tensor_add(flat, flat, rank.unsqueeze(2).to_broadcast([P, TG, PER_GROUP])), blk)

            def routing_weights(blk):
                rest = rt[:, 0, :].rearrange("p (t e) -> p t e", e=E)
                for t in range(TILES):
                    last = nc.vector.match_replace(rest[:, t, :], best[:, t, :], biased[:, t, :], -3.0e38)
                chain(last, blk)
                chain(nc.vector.tensor_tensor(rest, rest, biased[:, :, :], ALU.not_equal), blk)
                chain(nc.vector.tensor_mul(rest, rest, score[:, :, :]), blk)
                chain(nc.vector.tensor_reduce(small[:, 0:TILES], rest, AX, ALU.add), blk)
                chain(nc.vector.tensor_scalar_add(small[:, 0:TILES], small[:, 0:TILES], 1e-20), blk)
                chain(nc.vector.reciprocal(small[:, 4:4 + TILES], small[:, 0:TILES]), blk)
                chain(nc.vector.tensor_scalar_mul(small[:, 4:4 + TILES], small[:, 4:4 + TILES], ROUTE_SCALE), blk)
                nc.vector.tensor_mul(cw[:, :, :], rest, small[:, 4:4 + TILES].unsqueeze(2).to_broadcast([P, TILES, E]))\
                    .then_inc(S["cw_ready"], 1)

            def setup(ins):
                steps[0] += 1
                ins.then_inc(S["dve_chain"], 1)
                dve.wait_ge(S["dve_chain"], steps[0])

            dve.sem_inc(S["weighted"], NPAIR)
            dve.wait_ge(S["consts_in"], 16 * 7)
            setup(nc.vector.tensor_copy(pt_f[:, 0, :], pt_i[:, :]))
            setup(nc.vector.tensor_copy(onehot[:, :], cat_row[:, :]))
            setup(nc.vector.tensor_copy(vrep[:, :], bv[:, 1:2].to_broadcast([32, P])))
            setup(nc.vector.tensor_scalar(onehot[:, :], onehot[:, :], C["index"][0:CATS], None, ALU.is_equal))
            setup(nc.vector.tensor_scalar(pt_f[:, 1, :], pt_f[:, 0, :], 0.0, None, ALU.is_equal))
            setup(nc.vector.tensor_scalar(pt_f[:, 2, :], pt_f[:, 0, :], 1.0, None, ALU.is_equal))
            setup(nc.vector.tensor_add(pt_f[:, 3, :], pt_f[:, 1, :], pt_f[:, 2, :]))
            setup(nc.vector.tensor_scalar(pt_f[:, 3, :], pt_f[:, 3, :], -1.0, 1.0, ALU.mult, ALU.add))
            wide = [P, NSEQ // SPT, SEQ]
            tmp = s_t[:, 0:2, :].rearrange("p a (n l) -> p (a n) l", l=SEQ)
            for k in range(3):
                is_k = pt_f[:, 1 + k, :]
                mask = C[f"neg{k}"].unsqueeze(1).to_broadcast(wide)
                setup(nc.vector.tensor_mul(neg[:, :, :] if k == 0 else tmp, mask, is_k.unsqueeze(2).to_broadcast(wide)))
                if k:
                    nc.vector.tensor_add(neg[:, :, :], neg[:, :, :], tmp)
                    setup(nc.vector.scalar_tensor_tensor(cnt[:, k % 2, :], is_k, C["count"][:, k:k + 1],
                                                         cnt[:, (k + 1) % 2, :], ALU.mult, ALU.add))
                else:
                    setup(nc.vector.tensor_scalar(cnt[:, 0, :], is_k, C["count"][:, 0:1], None, ALU.mult))
            setup(nc.vector.tensor_copy(small[:, 0:1], small[:, 0:1]) if False else nc.vector.memset(small[:, :], 0.0))
            assert steps[0] == CHAIN_SETUP, steps[0]
            dve.wait_ge(S["setup"], 2)
            for p in range(UNITS):
                attention_step(p, 0)
            dve.wait_ge(S["x2_ready"], 1)
            nc.vector.tensor_copy(x2[:, :], x2_next[:, :]).then_inc(S["x2_moved"], 1)

            def experts(b, following):
                for p in range(UNITS):
                    dve.wait_ge(S["silu_done"], b * UNITS + p + 1)
                    if p < NPAIR:
                        dve.wait_ge(cwb_in[p % NCW], b * (16 * NPAIR // NCW) + 16 * (p // NCW + 1))
                        nc.vector.tensor_mul(act_w[:, p % 2, :], G[p % 2][:, :], cwb[:, p % NCW, :])\
                            .then_inc(S["weighted"], 1)
                    n = P if p < NPAIR else F
                    dve.wait_ge(S["up_done"], b * UNITS + p + 1)
                    if p < NPAIR:
                        dve.wait_ge(S["weighted"], (b + 1) * NPAIR + p + 1)
                    if p >= 2:
                        dve.wait_ge(S["lo_ready"], b * UNITS + p - 1)
                    nc.vector.tensor_mul(hid[0:n, p % 2, :], act_w[0:n, p % 2, :], U[p % 2][0:n, :])\
                        .then_inc(S["hid_ready"], 1)
                    if following is not None:
                        attention_step(p, following)
                dve.wait_ge(S["down_done"], b * UNITS + UNITS)
                dve.wait_ge(S["y_free"], b * 16 + 16)
                dve.wait_ge(S["x2_moved"], b + 1)
                nc.vector.tensor_add(y[:, :], Y[:, :], x2[:, :]).then_inc(S["y_ready"], 1)
                dve.wait_ge(S["y_ready"], b + 1)
                dve.sem_inc(S["sum_free"], 1)
                if following is not None:
                    dve.wait_ge(S["x2_ready"], b + 2)
                    nc.vector.tensor_copy(x2[:, :], x2_next[:, :]).then_inc(S["x2_moved"], 1)

            with dve.Fori(0, NBLK - 1) as b:
                experts(b, b + 1)
            experts(NBLK - 1, None)

        @block.tensor
        def _(pe):
            def mm(dst, lhsT, rhs, **k):
                k.setdefault("start", True)
                k.setdefault("stop", True)
                return nc.tensor.matmul(dst, lhsT, rhs, **k)

            def attention_step(p, blk):
                if p == 0:
                    pe.wait_ge(S["xf_in"], blk * 16 + 16)
                    wait(pe, "cwT_ready", blk)
                    mm(A0[0:32, :], W["w1"], xf[:, :]).then_inc(S["hidden_ps"], 1)
                elif p == 2:
                    pe.wait_ge(S["tanh_done"], blk + 1)
                    mm(A1[:, :], vrep[:, :], th).then_inc(S["score_ps"], 1)
                elif p == 6:
                    pe.wait_ge(S["xt_in"], blk * 16 + 16)
                    pe.wait_ge(S["pool_prob"], blk + 1)
                    for t in range(TILES):
                        last = mm(A0[:, bass.ts(t, P)], xt[:, t, :], pool_pt[:, t, :, :].rearrange("p s j -> p (s j)"))
                    last.then_inc(S["pooled_ps"], 1)
                elif p == 8:
                    pe.wait_ge(S["h_ready"], blk + 1)
                    mm(A1[:, :], W["kv"], h_feat[:, :]).then_inc(S["ckv_ps"], 1)
                    mm(A2[:, :], W["q"], h_feat[:, :]).then_inc(S["q_ps"], 1)
                elif p == 10:
                    pe.wait_ge(S["ckv_ready"], blk + 1)
                    for ps, half in ((A0, slice(0, ROPE)), (A1, slice(ROPE, 2 * ROPE))):
                        mm(ps[0:ROPE, :], W["qr"][:, half], h_feat[:, :])
                        last = mm(ps[ROPE:2 * ROPE, :], W["kr"][:, half], ckv[:, :])
                    last.then_inc(S["rope_ps"], 1)
                    pe.wait_ge(S["q_ready"], blk + 1)
                    mm(A2[:, :], W["k"], ckv[:, :]).then_inc(S["k_ps"], 1)
                elif p == 12:
                    pe.wait_ge(S["rope_ready"], blk + 1)
                    for t in range(TILES):
                        last = mm(A0[:, bass.ts(t, P)], ckv[:, bass.ts(t, P)], W["v"])
                    last.then_inc(S["v_ps"], 1)
                    for s in range(SPB):
                        t, r = divmod(s, SPT)
                        last = mm(A1[32 * r:32 * r + 32, bass.ts(t, SEQ)], qk_rope[:, 0, bass.ts(s, SEQ)],
                                  qk_rope[:, 1, bass.ts(s, SEQ)])
                    last.then_inc(S["rope_score_ps"], 1)
                elif 14 <= p < 18:
                    t = p - 14
                    ps = (A2, A0)[t % 2]
                    if t == 0:
                        pe.wait_ge(S["k_ready"], blk + 1)
                    elif t == 1:
                        pe.wait_ge(S["v_ready"], blk + 1)
                    else:
                        pe.wait_ge(S["biased_tile"], blk * TILES + t - 1)
                    for g in range(NG):
                        for r in range(SPT):
                            tok = bass.ts(t * SPT + r, SEQ)
                            last = mm(ps[32 * r:32 * r + 32, bass.ts(g, P)], q_grp[:, g, tok], k_blk[:, :, tok])
                    last.then_inc(S["score_tile_ps"], 1)
                if 19 <= p < 23:
                    t = p - 19
                    pe.wait_ge(S["prob_tile"], blk * TILES + t + 1)
                    if t == 0:
                        pe.wait_ge(S["rope_mask_ready"], blk + 1)
                    else:
                        pe.wait_ge(S["probT_ready"], blk * TILES + t)
                    for g in range(NG):
                        last = nc.tensor.transpose(A1[:, bass.ts(g, P)], s_t[:, t, bass.ts(g, P)], C["ident"])
                    last.then_inc(S["probT_ps"], 1)
                if 20 <= p < 24:
                    t = p - 20
                    pe.wait_ge(S["probT_ready"], blk * TILES + t + 1)
                    if t >= 2:
                        pe.wait_ge(S["att_ready"], blk * TILES + t - 1)
                    else:
                        pe.wait_ge(S["biased_tile"], blk * TILES + TILES)
                    ps = (A0, A2)[t % 2]
                    for g in range(NG):
                        for r in range(SPT):
                            last = mm(ps[32 * r:32 * r + 32, bass.ts(g, HG * VC)],
                                      pt_sb[:, t % 2, g * P + 32 * r:g * P + 32 * r + 32], v_blk[:, t, r, g, :])
                    last.then_inc(S["av_ps"], 1)
                elif p == 24:
                    pe.wait_ge(S["att_ready"], blk * TILES + TILES)
                    for t in range(TILES):
                        last = nc.tensor.transpose(A1[:, bass.ts(t, P)], att[:, t, :, :].rearrange("p h d -> p (h d)"),
                                                   C["ident"])
                    last.then_inc(S["attT_ps"], 1)
                elif p == 25:
                    pe.wait_ge(S["attT_ready"], blk + 1)
                    mm(A0[:, :], W["o"], att_feat[:, :]).then_inc(S["wo_ps"], 1)
                elif p == 26:
                    hot = onehot[:, bass.ds(blk * SPB, SPB)].unsqueeze(2).to_broadcast([CATS, SPB, SEQ])
                    mm(A1[:, :], cat_bias[:, :], hot, stop=False)
                    pe.wait_ge(S["x2_ready"], blk + 1)
                    pe.wait_ge(S["wcat_in"], blk * (16 * SPB) + 16 * SPB)
                    for s in range(SPB):
                        tok = bass.ts(s, SEQ)
                        last = mm(A1[:, tok], wcat[:, s, :], x2_next[:, tok], start=False, stop=(s == SPB - 1))
                    last.then_inc(S["c2_ps"], 1)
                elif p == 27:
                    pe.wait_ge(S["c2_ready"], blk + 1)
                    for t in range(TILES):
                        last = mm(A2[:, bass.ts(t, E)], c2[:, bass.ts(t, P)], W["gate"])
                    last.then_inc(S["gate_ps"], 1)
                elif p == 32:
                    pe.wait_ge(S["cw_ready"], blk + 1)
                    for t in range(0, TILES, 2):
                        last = nc.tensor.transpose(A0[:, bass.ts(t // 2, P)], cw[:, t:t + 2, :].rearrange("p t e -> p (t e)"),
                                                   C["ident"])
                    last.then_inc(S["cwT_ps"], 1)

            pe.wait_ge(S["consts_in"], 16 * 7)
            pe.wait_ge(S["dve_chain"], CHAIN_SETUP)
            pe.wait_ge(S["setup"], 2)
            for p in range(UNITS):
                attention_step(p, 0)
            pe.wait_ge(S["split_lo"], NSPLIT + 1)
            pe.sem_inc(S["sum_free"], 1)

            def three(dst, w_hi, w_lo, m_hi, m_lo, first, final):
                mm(dst, w_hi, m_hi, start=first, stop=False)
                mm(dst, w_lo, m_hi, start=False, stop=False)
                return mm(dst, w_hi, m_lo, start=False, stop=final)

            def experts(b, following):
                pe.wait_ge(S["c_lo_ready"], b + 1)

                def down(p):
                    n = P if p < NPAIR else F
                    pe.wait_ge(S["lo_ready"], b * UNITS + p + 1)
                    if p == 0:
                        pe.wait_ge(S["sum_free"], b + 1)
                    three(Y[:, :], wd_hi[0:n, p, :], wd_lo[0:n, p, :], hid_hi[0:n, p % 2, :], hid_lo[0:n, p % 2, :],
                          p == 0, p == UNITS - 1).then_inc(S["down_done"], 1)

                for p in range(UNITS):
                    m = P if p < NPAIR else F
                    if p >= 2:
                        pe.wait_ge(S["weighted"], (b + 1) * NPAIR + p - 1)
                    three(G[p % 2][0:m, :], wg_hi[:, p, 0:m], wg_lo[:, p, 0:m], c_hi[:, :], c_lo[:, :], True, True)\
                        .then_inc(S["gate_done"], 1)
                    if p >= 2:
                        pe.wait_ge(S["hid_ready"], b * UNITS + p - 1)
                    three(U[p % 2][0:m, :], wu_hi[:, p, 0:m], wu_lo[:, p, 0:m], c_hi[:, :], c_lo[:, :], True, True)\
                        .then_inc(S["up_done"], 1)
                    if p >= 2:
                        down(p - 2)
                    if following is not None:
                        attention_step(p, following)
                down(UNITS - 2)
                down(UNITS - 1)

            with pe.Fori(0, NBLK - 1) as b:
                experts(b, b + 1)
            experts(NBLK - 1, None)


def kernel(x, itok_B_0_2, itok_B_0_63, L0_cond_W1, L0_cond_b1, L0_cond_v, L0_attn_W_kv_down, L0_attn_W_k_up,
           L0_attn_W_v_up, L0_attn_W_q, L0_attn_W_q_rope, L0_attn_W_k_rope, L0_attn_W_o, L0_cond2_W, L0_cond2_b,
           L0_ffn_gate_w, L0_ffn_gate_bias, L0_ffn_We_gate, L0_ffn_We_up, L0_ffn_We_down, L0_ffn_Ws_gate,
           L0_ffn_Ws_up, L0_ffn_Ws_down):
    import concourse.bacc as bacc
    from concourse.bass_utils import run_bass_kernel_spmd

    def swapped(a):
        a = np.asarray(a)
        return np.concatenate([a, a[:, ROPE // 2:], a[:, :ROPE // 2]], 1)

    def experts_in(a):
        return np.ascontiguousarray(np.transpose(np.asarray(a), (1, 0, 2)).reshape(D, E * F))

    tokens = np.asarray(x).reshape(NSEQ * SEQ, D)
    arrays = {
        "x_tok": tokens.reshape(NBLK * TILES, P, D).transpose(1, 0, 2),
        "x_feat": tokens.T,
        "prompt": np.repeat(np.asarray(itok_B_0_2).reshape(NSEQ // SPT, SPT).T, SEQ, axis=0),
        "cats": np.asarray(itok_B_0_63).reshape(1, NSEQ),
        "cond_w": np.asarray(L0_cond2_W).reshape(CATS * D, D),
        "cond_b": np.asarray(L0_cond2_b),
        "weights": np.concatenate([np.asarray(a) for a in (
            L0_attn_W_kv_down, L0_attn_W_q, L0_attn_W_k_up, L0_attn_W_v_up, L0_attn_W_o, swapped(L0_attn_W_q_rope),
            swapped(L0_attn_W_k_rope), L0_cond_W1, np.asarray(L0_ffn_gate_w).T)], 1),
        "consts": shape_constants(),
        "b1v": np.stack([np.asarray(L0_cond_b1), np.asarray(L0_cond_v)], 1),
        "gate_bias": np.asarray(L0_ffn_gate_bias).reshape(1, E),
        "we_gate": experts_in(L0_ffn_We_gate),
        "we_up": experts_in(L0_ffn_We_up),
        "we_down": np.asarray(L0_ffn_We_down).reshape(NPAIR, 2 * F, D).transpose(1, 0, 2).reshape(2 * F, NPAIR * D),
        "ws_gu": np.concatenate([np.asarray(L0_ffn_Ws_gate), np.asarray(L0_ffn_Ws_up)], 1),
        "ws_down": np.asarray(L0_ffn_Ws_down),
    }
    nc = bacc.Bacc("TRN2", target_bir_lowering=False, num_devices=1)
    feeds, args = {}, []
    for name, a in arrays.items():
        a = np.ascontiguousarray(a)
        feeds[f"in_{name}"] = a
        args.append(nc.dram_tensor(f"in_{name}", a.shape, mybir.dt.from_np(a.dtype), kind="ExternalInput").ap())
    result = nc.dram_tensor("out_feat", (D, NSEQ * SEQ), F32, kind="ExternalOutput").ap()
    adaln_attention_moe(nc, *args, result)
    got = run_bass_kernel_spmd(nc, [feeds], core_ids=[0]).results[0]["out_feat"]
    return np.ascontiguousarray(got.T.reshape(NSEQ, SEQ, D))
```

```python
import numpy as np
import concourse.bass as bass
from concourse import mybir
from concourse.alu_op_type import AluOpType as ALU
from contextlib import ExitStack

F32 = mybir.dt.float32
F32R = mybir.dt.float32r
I32 = mybir.dt.int32
ACT = mybir.ActivationFunctionType
AX = mybir.AxisListType.X

P = 128
D = 128
SEQ = 32
NSEQ = 128
HEADS, HD = 16, 8
ROPE = 32
TOK = 512
NBLK = NSEQ * SEQ // TOK
TILES = TOK // P
SPT = P // SEQ
SPB = TOK // SEQ
CATS = 64
E, F = 64, 64
GROUPS, PER_GROUP, TOP_GROUPS, TOP_K = 8, 8, 4, 8
ROUTE_SCALE = 2.5
NPAIR = E // 2
UNITS = NPAIR + 1
ATT_SCALE = 1.0 / float(np.sqrt(HD + ROPE))
MASKED = -1.0e30
HG = 4
NG = HEADS // HG
VC = HD + 1

W_COLS, W_TOTAL = {}, 0
for _n, _w in (("kvT", D), ("q", D), ("k", D), ("v", D), ("kr", 2 * ROPE), ("o", D), ("qr", 2 * ROPE),
               ("w1", 32), ("b1", 1), ("vcol", 1), ("gate", E)):
    W_COLS[_n] = (W_TOTAL, _w)
    W_TOTAL += _w
C_COLS, C_TOTAL = {}, 0
for _n, _w in (("ident", P), ("head_of_group", HG), ("group", NG), ("causal", SEQ), ("neg0", SEQ), ("neg1", SEQ),
               ("neg2", SEQ), ("count", 3), ("rotary", SEQ), ("lower", GROUPS * GROUPS), ("index", 1)):
    C_COLS[_n] = (C_TOTAL, _w)
    C_TOTAL += _w


def shape_constants():
    c = np.zeros((P, C_TOTAL), np.float32)

    def col(name):
        a, w = C_COLS[name]
        return c[:, a:a + w]

    p = np.arange(P)
    j = (p % SEQ)[:, None]
    l = np.arange(SEQ)[None, :]
    col("ident")[:] = np.eye(P)
    col("head_of_group")[:] = (p % 32 // HD)[:, None] == np.arange(HG)
    col("group")[:] = (p // 32)[:, None] == np.arange(NG)
    col("causal")[:] = np.where(l <= j, 0.0, MASKED)
    for name, seen in (("neg0", l <= j), ("neg1", l >= j), ("neg2", l != j)):
        col(name)[:] = np.where(seen, 0.0, MASKED)
        col("count")[:, int(name[-1])] = seen.sum(1)
    inv = (1.0 / np.float32(10000.0) ** (np.arange(0, ROPE, 2, dtype=np.float32) / ROPE)).astype(np.float32)
    angle = np.outer(inv, np.arange(SEQ, dtype=np.float32)).astype(np.float32)
    half = p % ROPE % (ROPE // 2)
    sign = np.where(p % ROPE < ROPE // 2, -1.0, 1.0)[:, None]
    col("rotary")[:] = np.where((p < 2 * ROPE)[:, None], np.cos(angle)[half], np.sin(angle)[half] * sign)
    g = np.arange(GROUPS)
    col("lower")[:] = (g[None, :] < g[:, None]).reshape(1, -1)
    col("index")[:, 0] = p
    return c


def adaln_attention_moe(nc, x_tok, x_feat, prompt, cats, cond_w, cond_b, weights, consts, gate_bias,
                        we_gate, we_up, we_down, ws_gu, ws_down, out):
    ctx = ExitStack()
    with ctx:
        def sb(name, shape, dt=F32):
            return ctx.enter_context(nc.sbuf_tensor(name, shape, dt))

        def sem(name):
            return ctx.enter_context(nc.semaphore(name))

        w = sb("w", [P, W_TOTAL])
        c = sb("c", [P, C_TOTAL])
        W = {n: w[:, a:a + k] for n, (a, k) in W_COLS.items()}
        C = {n: c[:, a:a + k] for n, (a, k) in C_COLS.items()}
        wg_hi, wg_lo = sb("wg_hi", [P, UNITS, P], F32R), sb("wg_lo", [P, UNITS, P], F32R)
        wu_hi, wu_lo = sb("wu_hi", [P, NPAIR, P], F32R), sb("wu_lo", [P, NPAIR, P], F32R)
        wd_hi, wd_lo = sb("wd_hi", [P, UNITS, D], F32R), sb("wd_lo", [P, UNITS, D], F32R)
        k_w, v_w = sb("k_w", [P, D]), sb("v_w", [P, D])
        rope_w = sb("rope_w", [P, P])
        vrep = sb("vrep", [P, TILES, SEQ])
        gbias = sb("gbias", [P, E])
        cat_row = sb("cat_row", [CATS, NSEQ], I32)
        cat_bias = sb("cat_bias", [P, NSEQ])

        xf = sb("xf", [P, TOK])
        s_t = sb("s_t", [P, TILES, HEADS * SEQ])
        small = sb("small", [P, 16])
        h_feat = sb("h_feat", [P, TOK])
        q_grp = sb("q_grp", [P, NG, TOK])
        k_blk = sb("k_blk", [P, HG, TOK])
        wcat = k_blk[:, :, :].rearrange("p a b -> p (a b)").rearrange("p (s h) -> p s h", h=D)
        v_blk = sb("v_blk", [P, TILES, SPT, NG, HG * VC])
        pt_sb = sb("pt_sb", [P, 2, NG * P])
        rot = pt_sb[0:2 * ROPE]
        rope_sum = sb("rope_sum", [2 * ROPE, TOK])
        k_rope = sb("k_rope", [ROPE, TOK])
        rope_mask = sb("rope_mask", [P, TILES, SEQ])
        head_max = sb("head_max", [P, TILES, HEADS])
        rden = sb("rden", [P, TILES, HEADS])
        att = sb("att", [P, TILES, HEADS, HD])
        att_feat = h_feat
        x2_next = sb("x2_next", [P, TOK])
        c2_tok = att[:, :, :, :].rearrange("p t h d -> p (t h d)")
        c2 = sb("c2", [P, TOK])
        score = sb("score", [P, TILES, E])
        biased = sb("biased", [P, TILES, E])
        rt = sb("rt", [P, 3, TILES * E])
        best = sb("best", [P, TILES, 8])
        cw = sb("cw", [P, TILES, E])
        cw_feat = sb("cw_feat", [2 * E, TOK // 2])

        c_hi, c_lo = sb("c_hi", [P, TOK], F32R), sb("c_lo", [P, TOK], F32R)
        x2 = sb("x2", [P, TOK])
        NCW = 4
        NH = 3
        cwb = sb("cwb", [P, NCW, TOK])
        act_w = sb("act_w", [P, NH, TOK])
        hid = sb("hid", [P, NH, TOK])
        hid_hi, hid_lo = sb("hid_hi", [P, NH, TOK], F32R), sb("hid_lo", [P, NH, TOK], F32R)
        y = sb("y", [P, TOK])

        stage = cwb
        xf_in = [k_blk[:, i, :] for i in range(4)] + [xf[:, :], x2_next[:, :], c2_tok, h_feat[:, :]]
        xt_in = [q_grp[:, i, :] for i in range(4)] + [act_w[:, 2, :], hid[:, 2, :], y[:, :],
                                                      rt[:, 0:2, :].rearrange("p a n -> p (a n)")]
        hidden = s_t[:, 0:2, :].rearrange("p a n -> p (a n)").rearrange("p (i n) -> p i n", n=P)
        pooled = s_t[:, 2:4, :]
        pool_pt = pt_sb[:, :, :].rearrange("p i (t s j) -> p i t s j", t=TILES, s=SPT)
        tiles32 = "p a (n l) -> p (a n) l"
        neg = act_w[:, 0:2, :].rearrange(tiles32, l=SEQ)
        pool_p = hid[:, 0:2, :].rearrange(tiles32, l=SEQ)
        mask_tmp = hid[:, 0:2, :].rearrange(tiles32, l=SEQ)
        stats = x2[:, 0:8 * NSEQ // SPT].rearrange("p (k n) -> p k n", k=8)
        pt_i = best[:, :, :].rearrange("p a n -> p (a n)")[:, 0:NSEQ // SPT].bitcast(I32)
        cat_table = c2[0:CATS, 0:D]
        onehot = c2[0:CATS, D:D + NSEQ]

        h_dram = nc.dram_tensor("pooled_scratch", [P, NSEQ * SEQ], F32).ap()
        cw_dram = nc.dram_tensor("cw_scratch", [E, NSEQ * SEQ], F32).ap()

        def bank(name):
            return ctx.enter_context(nc.psum_tensor(name, [P, 512], F32))

        A0, A1, A2 = bank("A0"), bank("A1"), bank("A2")
        G = [bank("G0"), bank("G1")]
        U = [bank("U0"), bank("U1")]
        Y = bank("Y")

        S = {}
        for name in """consts_in xf_in0 xf_in1 xt_in0 xt_in1 stage_in0 stage_in1 stage_in2 stage_in3
                small_in split_hi split_lo setup fold_ps folded cat_ps hidden_ps tanh_done score_ps pool_sub pool_exp
                pool_prob pooled_ps pooled_ready h_stored0 h_stored1
                h_in res_in krope_in wcat_in cw_stored y_free cwb_in0 cwb_in1 cwb_in2 cwb_in3
                q_ps rope_ps k_ps q_ready rot_ready rope_summed k_ready v_ps v_ready rope_score_ps rope_mask_ready
                score_tile_ps biased_tile sub_tile prob_tile probT_ps probT_ready av_ps att_ready attT_ps attT_ready
                wo_ps x2_ready c2tok_ps c2tok_ready c2_ps c2_ready gate_ps tanh_gate score_ready biased_ready compared ties_masked beaten_ready cw_ready cwT_ps cwT_ready
                dve_chain c_hi_ready c_lo_ready x2_moved gate_done silu_done up_done weighted hid_ready hi_ready
                lo_ready down_done y_ready sum_free""".split():
            S[name] = sem(name)
        stage_in = [S[f"stage_in{i}"] for i in range(4)]
        cwb_in = [S[f"cwb_in{i}"] for i in range(4)]

        def wait(eng, name, value):
            if not (isinstance(value, int) and value <= 0):
                eng.wait_ge(S[name], value)

        HALF = NBLK // 2
        CONSTS = 6 * 16
        NSPLIT = 24
        EARLY = 13
        CHAIN_SETUP = 13
        CHAIN_POOL = 10
        CHAIN_BASE = CHAIN_SETUP + CHAIN_POOL
        CHAIN = 24
        CWT = 31
        block = ctx.enter_context(nc.Block())

        @block.sync
        def _(sp):
            for dst, src in ((c[:, :], consts), (w[:, :], weights), (pt_i, prompt),
                             (cat_row[:, :], cats.to_broadcast([CATS, NSEQ])), (cat_table, cond_b),
                             (gbias[:, :], gate_bias.to_broadcast([P, E]))):
                sp.dma_start(dst, src).then_inc(S["consts_in"], 16)

            def stage_load(i):
                if i >= 4:
                    sp.wait_ge(S["split_lo"], i - 3)
                if i < NSPLIT:
                    src = (we_gate, we_up, we_down)[i // 8][:, bass.ts(i % 8, TOK)]
                    sp.dma_start(stage[:, i % 4, :], src).then_inc(stage_in[i % 4], 16)
                else:
                    sp.dma_start(stage[:, 0, 0:2 * F], ws_gu).then_inc(stage_in[0], 16)
                    sp.dma_start(stage[0:F, 0, 2 * F:2 * F + D], ws_down).then_inc(S["small_in"], 16)

            def attention_loads(p, blk):
                if p == 0:
                    if not isinstance(blk, int):
                        wait(sp, "wo_ps", blk)
                        sp.dma_start(h_feat[:, :], h_dram[:, bass.ds(blk * TOK, TOK)]).then_inc(S["h_in"], 16)
                    wait(sp, "x2_ready", blk)
                    sp.dma_start(xf[:, :], x_feat[:, bass.ds(blk * TOK, TOK)]).then_inc(S["res_in"], 16)
                elif p == 4:
                    sp.wait_ge(S["rope_summed"], blk + 1)
                    sp.dma_start(k_rope[:, :], rope_sum[ROPE:2 * ROPE, :]).then_inc(S["krope_in"], 16)
                elif 13 <= p < 21:
                    for s in range(2 * (p - 13), 2 * (p - 13) + 2):
                        cat = sp.value_load(cat_row[0:1, bass.ds(blk * SPB + s, 1)], min_val=0, max_val=CATS - 1)
                        if s == 0:
                            sp.wait_ge(S["score_tile_ps"], blk * TILES + TILES)
                        sp.dma_start(wcat[:, s, :], cond_w[bass.ds(cat * D, D), :]).then_inc(S["wcat_in"], 16)
                elif p == 32:
                    sp.wait_ge(S["cwT_ready"], blk + 1)
                    dst = cw_dram[:, bass.ds(blk * TOK, TOK)].rearrange("e (u two n) -> e u two n", two=2, n=P)
                    for i in range(2):
                        sp.dma_start(dst[:, :, i, :], cw_feat[E * i:E * i + E, :].rearrange("e (u n) -> e u n", n=P))\
                            .then_inc(S["cw_stored"], 16)

            for j in range(2):
                for i in range(HALF * j, HALF * j + HALF):
                    sp.dma_start(xf_in[i], x_feat[:, bass.ts(i, TOK)]).then_inc(S[f"xf_in{j}"], 16)
            for i in range(4):
                stage_load(i)
            for j in range(2):
                for i in range(HALF * j, HALF * j + HALF):
                    sp.dma_start(xt_in[i].rearrange("p (t d) -> p t d", d=D), x_tok[:, bass.ts(i, TILES), :])\
                        .then_inc(S[f"xt_in{j}"], 16)
            for i in range(4, EARLY + 4):
                stage_load(i)
            sp.wait_ge(S["hidden_ps"], 2)
            attention_loads(0, 0)
            attention_loads(4, 0)
            for p in range(UNITS):
                if EARLY + 4 + p <= NSPLIT:
                    stage_load(EARLY + 4 + p)
                if p > 4:
                    attention_loads(p, 0)
            for i in range(2):
                sp.wait_ge(S[f"h_stored{i}"], 16 * (HALF + i - 1))

            def experts_loads(b, following):
                for p in range(UNITS):
                    if following is not None:
                        attention_loads(p, following)
                    if p < NPAIR:
                        sp.wait_ge(S["weighted"], (b + 1) * NPAIR + max(0, p - NCW + 1))
                        if p == 0:
                            sp.wait_ge(S["cw_stored"], (b + 1) * 32)
                        src = cw_dram[2 * p:2 * p + 2, bass.ds(b * TOK, TOK)].unsqueeze(1).to_broadcast([2, F, TOK])
                        sp.dma_start(cwb[:, p % NCW, :], src).then_inc(cwb_in[p % NCW], 16)

            sp.wait_ge(S["split_lo"], NSPLIT + 1)
            with sp.Fori(0, NBLK - 1) as b:
                experts_loads(b, b + 1)
            experts_loads(NBLK - 1, None)
            sp.wait_ge(S["y_free"], 16 * NBLK + 16)

        @block.scalar
        def _(act):
            def attention_step(p, blk):
                if 1 <= p < 5:
                    if p == 1:
                        act.wait_ge(S["q_ps"], blk + 1)
                    nc.scalar.mul(q_grp[:, p - 1, :], A2[:, :], C["group"][:, p - 1:p]).then_inc(S["q_ready"], 1)
                elif 5 <= p < 9:
                    s = p - 5
                    if s == 0:
                        act.wait_ge(S["v_ps"], blk + 1)
                    for r in range(HG):
                        src = A0[32 * s:32 * s + 32, :].rearrange("p (t c r d) -> p t c r d", t=TILES, c=NG, r=HG)
                        dst = v_blk[32 * r:32 * r + 32, :, s, :, r * VC:r * VC + HD]
                        last = nc.scalar.copy(dst, src[:, :, :, r, :])
                    last.then_inc(S["v_ready"], 1)
                elif p == 10:
                    for t in range(TILES):
                        act.wait_ge(S["sub_tile"], blk * TILES + t + 1)
                        nc.scalar.activation(s_t[:, t, :], s_t[:, t, :], ACT.Exp, scale=ATT_SCALE)\
                            .then_inc(S["prob_tile"], 1)
                elif 12 <= p < 16:
                    t = p - 12
                    act.wait_ge(S["probT_ps"], blk * TILES + t + 1)
                    if t >= 2:
                        act.wait_ge(S["av_ps"], blk * TILES + t - 1)
                    nc.scalar.copy(pt_sb[:, t % 2, :], A1[:, :]).then_inc(S["probT_ready"], 1)
                elif p == 17:
                    act.wait_ge(S["attT_ps"], blk + 1)
                    nc.scalar.copy(att_feat[:, :], A1[:, :]).then_inc(S["attT_ready"], 1)
                elif p == 19:
                    act.wait_ge(S["c2tok_ps"], blk + 1)
                    nc.scalar.copy(c2_tok, A1[:, :]).then_inc(S["c2tok_ready"], 1)
                elif p == 21:
                    act.wait_ge(S["gate_ps"], blk + 1)
                    nc.scalar.activation(score[:, :, :].rearrange("p t e -> p (t e)"), A2[:, 0:TILES * E], ACT.Tanh,
                                         scale=0.5).then_inc(S["tanh_gate"], 1)
                    act.wait_ge(S["tanh_gate"], blk + 1)
                    nc.scalar.activation(score[:, :, :].rearrange("p t e -> p (t e)"),
                                         score[:, :, :].rearrange("p t e -> p (t e)"), ACT.Copy, bias=0.5,
                                         scale=0.5).then_inc(S["score_ready"], 1)
                elif p == CWT:
                    act.wait_ge(S["cwT_ps"], blk + 1)
                    wait(act, "cw_stored", blk * 32)
                    nc.scalar.copy(cw_feat[:, :], A0[:, 0:TOK // 2]).then_inc(S["cwT_ready"], 1)

            def switch(blk):
                wait(act, "gate_done", blk * UNITS)
                act.wait_ge(S["c2_ready"], blk + 1)
                nc.scalar.copy(c_hi[:, :], c2[:, :]).then_inc(S["c_hi_ready"], 1)

            def split(i):
                act.wait_ge(stage_in[i % 4], 16 * (i // 4 + 1))
                if i < NSPLIT:
                    hi = (wg_hi, wu_hi, wd_hi)[i // 8]
                    nc.scalar.copy(hi[:, 4 * (i % 8):4 * (i % 8) + 4, :].rearrange("p a b -> p (a b)"),
                                   stage[:, i % 4, :]).then_inc(S["split_hi"], 1)
                else:
                    act.wait_ge(S["small_in"], 16)
                    nc.scalar.copy(wg_hi[:, NPAIR, :], stage[:, 0, 0:2 * F])
                    nc.scalar.copy(wd_hi[0:F, NPAIR, :], stage[0:F, 0, 2 * F:2 * F + D]).then_inc(S["split_hi"], 1)

            act.sem_inc(S["y_free"], 16)
            act.wait_ge(S["consts_in"], CONSTS)
            act.wait_ge(S["fold_ps"], 1)
            nc.scalar.copy(k_w[:, :], A2[:, 0:D])
            nc.scalar.copy(v_w[:, :], A2[:, D:2 * D])
            for i in range(2):
                nc.scalar.copy(rope_w[:, 2 * ROPE * i:2 * ROPE * i + ROPE], W["qr"][:, bass.ts(i, ROPE)])
                last = nc.scalar.copy(rope_w[:, 2 * ROPE * i + ROPE:2 * ROPE * (i + 1)],
                                      A2[:, 2 * D + ROPE * i:2 * D + ROPE * (i + 1)])
            last.then_inc(S["folded"], 1)
            splits = iter(range(NSPLIT + 1))
            for j in range(2):
                act.wait_ge(S["hidden_ps"], j + 1)
                nc.scalar.activation(hidden[:, HALF * j:HALF * j + HALF, :].rearrange("p i n -> p (i n)"), G[j][:, :],
                                     ACT.Tanh, bias=W["b1"]).then_inc(S["tanh_done"], 1)
            act.wait_ge(S["cat_ps"], 1)
            nc.scalar.copy(cat_bias[:, :], Y[:, 0:NSEQ])
            for j in range(2):
                act.wait_ge(S["pool_sub"], j + 1)
                part = pool_p[:, HALF * TILES * j:HALF * TILES * (j + 1), :]
                nc.scalar.activation(part, part, ACT.Exp).then_inc(S["pool_exp"], 1)
                for _i in range(2):
                    split(next(splits))
            for i in range(NBLK):
                split(next(splits))
                act.wait_ge(S["pooled_ps"], i + 1)
                if i == 0:
                    nc.scalar.copy(h_feat[:, :], A0[:, :]).then_inc(S["pooled_ready"], 1)
                    continue
                if i >= 3:
                    act.wait_ge(S[f"h_stored{i % 2}"], 16 * ((i - 1) // 2))
                nc.scalar.copy(pooled[:, i % 2, :], (A0, A1)[i % 2][:, :]).then_inc(S["pooled_ready"], 1)
                act.wait_ge(S["pooled_ready"], i + 1)
                act.dma_start(h_dram[:, bass.ts(i, TOK)], pooled[:, i % 2, :]).then_inc(S[f"h_stored{i % 2}"], 16)
            split(next(splits))
            for p in range(UNITS):
                attention_step(p, 0)
                if EARLY + p <= NSPLIT:
                    split(next(splits))
            switch(0)

            def experts(b, following):
                def rounded(p):
                    act.wait_ge(S["hid_ready"], b * UNITS + p + 1)
                    if p >= NH:
                        act.wait_ge(S["down_done"], b * UNITS + p - NH + 1)
                    n = P if p < NPAIR else F
                    nc.scalar.copy(hid_hi[0:n, p % NH, :], hid[0:n, p % NH, :]).then_inc(S["hi_ready"], 1)

                for p in range(UNITS):
                    act.wait_ge(S["gate_done"], b * UNITS + p + 1)
                    if p < NPAIR:
                        nc.scalar.activation(G[p % 2][:, :], G[p % 2][:, :], ACT.Silu).then_inc(S["silu_done"], 1)
                    else:
                        act.wait_ge(S["hid_ready"], b * UNITS + p - NH + 1)
                        nc.scalar.activation(act_w[0:F, p % NH, :], G[p % 2][0:F, :], ACT.Silu)\
                            .then_inc(S["silu_done"], 1)
                    if p >= 1:
                        rounded(p - 1)
                    if following is not None:
                        attention_step(p, following)
                    if p == 4:
                        nc.scalar.copy(x2[:, :], x2_next[:, :]).then_inc(S["x2_moved"], 1)
                rounded(UNITS - 1)
                if following is not None:
                    switch(following)
                act.wait_ge(S["y_ready"], b + 1)
                act.dma_start(out[:, bass.ds(b * TOK, TOK)], y[:, :]).then_inc(S["y_free"], 16)

            with act.Fori(0, NBLK - 1) as b:
                experts(b, b + 1)
            experts(NBLK - 1, None)

        @block.gpsimd
        def _(pool):
            def attention_step(p, blk):
                if p == 1:
                    pool.wait_ge(S["rot_ready"], blk + 1)
                    nc.gpsimd.tensor_add(rope_sum[:, :], rot[:, 0, :], rot[:, 1, :]).then_inc(S["rope_summed"], 1)
                elif 6 <= p < 10:
                    t = p - 6
                    pool.wait_ge(S["biased_tile"], blk * TILES + t + 1)
                    s = s_t[:, t, :].rearrange("p (h k) -> p h k", k=SEQ)
                    nc.gpsimd.tensor_sub(s, s, head_max[:, t, :].unsqueeze(2).to_broadcast([P, HEADS, SEQ]))\
                        .then_inc(S["sub_tile"], 1)
                elif p == 22:
                    pool.wait_ge(S["score_ready"], blk + 1)
                    nc.gpsimd.tensor_add(biased[:, :, :], score[:, :, :],
                                         gbias[:, :].unsqueeze(1).to_broadcast([P, TILES, E])).then_inc(S["biased_ready"], 1)
                elif p == 25:
                    pool.wait_ge(S["compared"], blk + 1)
                    tie_rows = rt[:, 1, :].rearrange("p (t n) -> p t n", n=GROUPS * GROUPS)
                    nc.gpsimd.tensor_mul(tie_rows, tie_rows, C["lower"].unsqueeze(1).to_broadcast([P, TILES, GROUPS * GROUPS]))\
                        .then_inc(S["ties_masked"], 1)
                    pool.wait_ge(S["ties_masked"], blk + 1)
                    nc.gpsimd.tensor_add(rt[:, 0, :], rt[:, 0, :], rt[:, 1, :]).then_inc(S["beaten_ready"], 1)

            def split(i):
                pool.wait_ge(S["split_hi"], i + 1)
                if i < NSPLIT:
                    hi, lo = ((wg_hi, wg_lo), (wu_hi, wu_lo), (wd_hi, wd_lo))[i // 8]
                    hi, lo = (a[:, 4 * (i % 8):4 * (i % 8) + 4, :].rearrange("p a b -> p (a b)") for a in (hi, lo))
                    nc.gpsimd.tensor_sub(lo, stage[:, i % 4, :], hi.bitcast(F32)).then_inc(S["split_lo"], 1)
                else:
                    nc.gpsimd.tensor_sub(wg_lo[:, NPAIR, :], stage[:, 0, 0:2 * F], wg_hi[:, NPAIR, :].bitcast(F32))
                    nc.gpsimd.tensor_sub(wd_lo[0:F, NPAIR, :], stage[0:F, 0, 2 * F:2 * F + D],
                                         wd_hi[0:F, NPAIR, :].bitcast(F32)).then_inc(S["split_lo"], 1)

            pool.memset(pool_pt[:, :, :, :, :], 0.0)
            nc.gpsimd.memset(v_blk[:, :, :, :, :], 0.0).then_inc(S["setup"], 1)
            pool.wait_ge(S["setup"], 1)
            v_ones = v_blk[:, :, :, :, :].rearrange("p t s c m -> p (t s c) m")
            for r in range(HG):
                last = nc.gpsimd.memset(v_ones[32 * r:32 * r + 32, :, r * VC + HD:r * VC + VC], 1.0)
            last.then_inc(S["setup"], 1)
            pool.wait_ge(S["setup"], 2)
            for i in range(EARLY):
                split(i)
            for p in range(UNITS):
                attention_step(p, 0)
                if EARLY + p <= NSPLIT:
                    split(EARLY + p)

            def experts(b, following):
                for p in range(UNITS):
                    pool.wait_ge(S["hi_ready"], b * UNITS + p + 1)
                    if p >= NH:
                        pool.wait_ge(S["down_done"], b * UNITS + p - NH + 1)
                    n = P if p < NPAIR else F
                    nc.gpsimd.tensor_sub(hid_lo[0:n, p % NH, :], hid[0:n, p % NH, :],
                                         hid_hi[0:n, p % NH, :].bitcast(F32)).then_inc(S["lo_ready"], 1)
                    if following is not None:
                        attention_step(p, following)

            with pool.Fori(0, NBLK - 1) as b:
                experts(b, b + 1)
            experts(NBLK - 1, None)

        @block.vector
        def _(dve):
            steps = [0]

            def chain(ins, blk):
                steps[0] += 1
                ins.then_inc(S["dve_chain"], 1)
                dve.wait_ge(S["dve_chain"], CHAIN_BASE + blk * CHAIN + steps[0])

            def attention_step(p, blk):
                if p == 0:
                    steps[0] = 0
                    dve.wait_ge(S["rope_ps"], blk + 1)
                    for i in range(2):
                        rows = slice(2 * ROPE * i, 2 * ROPE * (i + 1))
                        last = nc.vector.tensor_mul(
                            rot[:, i, :].rearrange("p (s t) -> p s t", t=SEQ),
                            A0[rows, :].rearrange("p (s t) -> p s t", t=SEQ),
                            C["rotary"][rows].unsqueeze(1).to_broadcast([2 * ROPE, SPB, SEQ]))
                    last.then_inc(S["rot_ready"], 1)
                elif 1 <= p < 5:
                    h = p - 1
                    if h == 0:
                        dve.wait_ge(S["k_ps"], blk + 1)
                    nc.vector.tensor_scalar(k_blk[:, h, :], A1[:, :], C["head_of_group"][:, h:h + 1], None, ALU.mult)\
                        .then_inc(S["k_ready"], 1)
                elif p == 5:
                    dve.wait_ge(S["rope_score_ps"], blk + 1)
                    nc.vector.tensor_add(rope_mask[:, :, :], A2[:, 0:TILES * SEQ].rearrange("p (t k) -> p t k", k=SEQ),
                                         C["causal"].unsqueeze(1).to_broadcast([P, TILES, SEQ]))\
                        .then_inc(S["rope_mask_ready"], 1)
                elif 6 <= p < 10:
                    t = p - 6
                    if t == 0:
                        dve.wait_ge(S["rope_mask_ready"], blk + 1)
                    dve.wait_ge(S["score_tile_ps"], blk * TILES + t + 1)
                    s = s_t[:, t, :].rearrange("p (h k) -> p h k", k=SEQ)
                    chain(nc.vector.tensor_add(s, (A2, A1)[t % 2][:, :].rearrange("p (h k) -> p h k", k=SEQ),
                                               rope_mask[:, t, :].unsqueeze(1).to_broadcast([P, HEADS, SEQ])), blk)
                    nc.vector.tensor_reduce(head_max[:, t, :], s, AX, ALU.max).then_inc(S["biased_tile"], 1)
                elif 13 <= p < 17:
                    t = p - 13
                    ps = (A0, A2)[t % 2][:, 0:HEADS * VC].rearrange("p (h m) -> p h m", m=VC)
                    dve.wait_ge(S["av_ps"], blk * TILES + t + 1)
                    chain(nc.vector.reciprocal(rden[:, t, :], ps[:, :, HD]), blk)
                    nc.vector.tensor_mul(att[:, t, :, :], ps[:, :, 0:HD],
                                         rden[:, t, :].unsqueeze(2).to_broadcast([P, HEADS, HD]))\
                        .then_inc(S["att_ready"], 1)
                elif p == 18:
                    wait(dve, "x2_moved", blk)
                    dve.wait_ge(S["res_in"], 16 * blk + 16)
                    dve.wait_ge(S["wo_ps"], blk + 1)
                    nc.vector.tensor_add(x2_next[:, :], A0[:, :], xf[:, :]).then_inc(S["x2_ready"], 1)
                elif p == 20:
                    dve.wait_ge(S["c2_ps"], blk + 1)
                    nc.vector.tensor_add(c2[:, :].rearrange("p (s t) -> p s t", t=SEQ),
                                         A0[:, :].rearrange("p (s t) -> p s t", t=SEQ),
                                         cat_bias[:, bass.ds(blk * SPB, SPB)].unsqueeze(2).to_broadcast([P, SPB, SEQ]))\
                        .then_inc(S["c2_ready"], 1)
                elif p in ROUTING:
                    ROUTING[p](blk)

            flat = biased[:, :, :].rearrange("p t (g e) -> p (t g) e", e=PER_GROUP)
            TG = TILES * GROUPS
            rest = rt[:, 0, :].rearrange("p (t e) -> p t e", e=E)

            def sorted_pair(level, which):
                width, at = PER_GROUP >> (level + 1), TG * (PER_GROUP - (PER_GROUP >> level))
                return rt[:, which, at:at + TG * width].rearrange("p (n w) -> p n w", w=width), width

            def routing_pairs(blk):
                dve.wait_ge(S["biased_ready"], blk + 1)
                (large, width), (little, _) = sorted_pair(0, 0), sorted_pair(0, 1)
                nc.vector.tensor_tensor(large, flat[:, :, 0:width], flat[:, :, width:2 * width], ALU.max)
                chain(nc.vector.tensor_tensor(little, flat[:, :, 0:width], flat[:, :, width:2 * width], ALU.min), blk)
                merge(1, blk)

            def merge(level, blk):
                (large, width), (little, _) = sorted_pair(level, 0), sorted_pair(level, 1)
                (v, _), (low, _) = sorted_pair(level - 1, 0), sorted_pair(level - 1, 1)
                other = rt[:, 2, 0:TG * width].rearrange("p (n w) -> p n w", w=width)
                nc.vector.tensor_tensor(large, v[:, :, 0:width], v[:, :, width:2 * width], ALU.max)
                nc.vector.tensor_tensor(little, v[:, :, 0:width], v[:, :, width:2 * width], ALU.min)
                chain(nc.vector.tensor_tensor(other, low[:, :, 0:width], low[:, :, width:2 * width], ALU.max), blk)
                chain(nc.vector.tensor_tensor(little, little, other, ALU.max), blk)

            def routing_sums(blk):
                merge(2, blk)
                (large, _), (little, _) = sorted_pair(2, 0), sorted_pair(2, 1)
                chain(nc.vector.tensor_add(best[:, :, :].rearrange("p t g -> p (t g)"), large[:, :, 0], little[:, :, 0]),
                      blk)

            def routing_compare(blk):
                wide = [P, TILES, GROUPS, GROUPS]
                mine, others = best[:, :, :].unsqueeze(3).to_broadcast(wide), best[:, :, :].unsqueeze(2).to_broadcast(wide)
                above, ties = (rt[:, i, :].rearrange("p (t g o) -> p t g o", g=GROUPS, o=GROUPS) for i in (0, 1))
                nc.vector.tensor_tensor(above, others, mine, ALU.is_gt)
                nc.vector.tensor_tensor(ties, others, mine, ALU.is_equal).then_inc(S["compared"], 1)

            def routing_groups(blk):
                dve.wait_ge(S["beaten_ready"], blk + 1)
                rank = rt[:, 2, 0:TG]
                chain(nc.vector.tensor_reduce(rank, rt[:, 0, :].rearrange("p (n o) -> p n o", o=GROUPS), AX, ALU.add), blk)
                chain(nc.vector.tensor_scalar(rank, rank, float(TOP_GROUPS), MASKED, ALU.is_ge, ALU.mult), blk)
                chain(nc.vector.tensor_add(flat, flat, rank.unsqueeze(2).to_broadcast([P, TG, PER_GROUP])), blk)

            def routing_top(blk):
                for t in range(TILES):
                    last = nc.vector.max(best[:, t, :], biased[:, t, :])
                chain(last, blk)

            def routing_chosen(blk):
                for t in range(TILES):
                    last = nc.vector.match_replace(rest[:, t, :], best[:, t, :], biased[:, t, :], -3.0e38)
                chain(last, blk)
                chain(nc.vector.tensor_tensor(rest, rest, biased[:, :, :], ALU.not_equal), blk)
                chain(nc.vector.tensor_mul(rest, rest, score[:, :, :]), blk)

            def routing_weights(blk):
                chain(nc.vector.tensor_reduce(small[:, 0:TILES], rest, AX, ALU.add), blk)
                chain(nc.vector.tensor_scalar(small[:, 0:TILES], small[:, 0:TILES], 1e-20, 1.0 / ROUTE_SCALE, ALU.add,
                                              ALU.mult), blk)
                chain(nc.vector.reciprocal(small[:, 4:4 + TILES], small[:, 0:TILES]), blk)
                nc.vector.tensor_mul(cw[:, :, :], rest, small[:, 4:4 + TILES].unsqueeze(2).to_broadcast([P, TILES, E]))\
                    .then_inc(S["cw_ready"], 1)
                assert steps[0] == CHAIN, steps[0]

            ROUTING = {23: routing_pairs, 24: routing_sums, 25: routing_compare, 27: routing_groups, 28: routing_top,
                       29: routing_chosen, 30: routing_weights}

            def setup(ins):
                steps[0] += 1
                ins.then_inc(S["dve_chain"], 1)
                dve.wait_ge(S["dve_chain"], steps[0])

            dve.sem_inc(S["weighted"], NPAIR)
            nc.vector.memset(vrep[:, :, :], 0.0)
            dve.wait_ge(S["consts_in"], CONSTS)
            kind, is_kind, count = stats[:, 0, :], [stats[:, 1 + k, :] for k in range(3)], [stats[:, 4 + k, :] for k in range(2)]
            setup(nc.vector.tensor_copy(kind, pt_i))
            setup(nc.vector.tensor_copy(onehot, cat_row[:, :]))
            for t in range(TILES):
                rows = slice(SEQ * t, SEQ * t + SEQ)
                nc.vector.tensor_copy(vrep[rows, t, :], W["vcol"][rows].to_broadcast([SEQ, SEQ]))
            setup(nc.vector.tensor_scalar(onehot, onehot, C["index"][0:CATS], None, ALU.is_equal))
            setup(nc.vector.tensor_scalar(is_kind[0], kind, 0.0, None, ALU.is_equal))
            setup(nc.vector.tensor_scalar(is_kind[1], kind, 1.0, None, ALU.is_equal))
            setup(nc.vector.tensor_add(is_kind[2], is_kind[0], is_kind[1]))
            setup(nc.vector.tensor_scalar(is_kind[2], is_kind[2], -1.0, 1.0, ALU.mult, ALU.add))
            wide = [P, NSEQ // SPT, SEQ]
            for k in range(3):
                mask = C[f"neg{k}"].unsqueeze(1).to_broadcast(wide)
                setup(nc.vector.tensor_mul(neg if k == 0 else mask_tmp, mask, is_kind[k].unsqueeze(2).to_broadcast(wide)))
                if k:
                    nc.vector.tensor_add(neg, neg, mask_tmp)
                    setup(nc.vector.scalar_tensor_tensor(count[k % 2], is_kind[k], C["count"][:, k:k + 1],
                                                         count[(k + 1) % 2], ALU.mult, ALU.add))
                else:
                    setup(nc.vector.tensor_scalar(count[0], is_kind[0], C["count"][:, 0:1], None, ALU.mult))
            assert steps[0] == CHAIN_SETUP, steps[0]

            largest, total = stats[:, 6, :], stats[:, 7, :]

            def half(a, j):
                return a[:, HALF * TILES * j:HALF * TILES * (j + 1)]

            def over_row(a):
                return a.unsqueeze(2).to_broadcast([P, HALF * TILES, SEQ])

            for j in range(2):
                part = half(pool_p, j)
                dve.wait_ge(S["score_ps"], j + 1)
                setup(nc.vector.tensor_add(part, U[j][:, :].rearrange("p (n l) -> p n l", l=SEQ), half(neg, j)))
                setup(nc.vector.tensor_reduce(half(largest, j), part, AX, ALU.max))
                nc.vector.tensor_sub(part, part, over_row(half(largest, j))).then_inc(S["pool_sub"], 1)
            dve.wait_ge(S["setup"], 2)
            for j in range(2):
                part = half(pool_p, j)
                dve.wait_ge(S["pool_exp"], j + 1)
                setup(nc.vector.tensor_reduce(half(total, j), part, AX, ALU.add))
                setup(nc.vector.tensor_mul(half(total, j), half(total, j), half(count[0], j)))
                nc.vector.reciprocal(half(largest, j), half(total, j)).then_inc(S["dve_chain"], 1)
                steps[0] += 1
                dve.wait_ge(S["dve_chain"], steps[0])
                nc.vector.tensor_mul(part, part, over_row(half(largest, j))).then_inc(S["pool_prob"], 1)
                dve.wait_ge(S["pool_prob"], HALF * j + j + 1)
                for i in range(HALF * j, HALF * j + HALF):
                    if i >= 2:
                        dve.wait_ge(S["pooled_ps"], i - 1)
                    for s in range(SPT):
                        rows = slice(SEQ * s, SEQ * s + SEQ)
                        last = nc.vector.transpose(pool_pt[rows, i % 2, :, s, :], pool_p[rows, bass.ts(i, TILES), :])
                    last.then_inc(S["pool_prob"], 1)
            assert steps[0] == CHAIN_BASE, steps[0]

            for p in range(UNITS):
                if p == 6:
                    for i in range(2):
                        dve.wait_ge(S[f"h_stored{i}"], 16 * (HALF + i - 1))
                attention_step(p, 0)

            def switch(blk):
                dve.wait_ge(S["c_hi_ready"], blk + 1)
                nc.vector.tensor_sub(c_lo[:, :], c2[:, :], c_hi[:, :].bitcast(F32)).then_inc(S["c_lo_ready"], 1)

            switch(0)

            def experts(b, following):
                for p in range(UNITS):
                    dve.wait_ge(S["silu_done"], b * UNITS + p + 1)
                    if p < NPAIR:
                        dve.wait_ge(cwb_in[p % NCW], b * (16 * NPAIR // NCW) + 16 * (p // NCW + 1))
                        nc.vector.tensor_mul(act_w[:, p % NH, :], G[p % 2][:, :], cwb[:, p % NCW, :])\
                            .then_inc(S["weighted"], 1)
                        dve.wait_ge(S["up_done"], b * NPAIR + p + 1)
                        dve.wait_ge(S["weighted"], (b + 1) * NPAIR + p + 1)
                    if p >= NH:
                        dve.wait_ge(S["lo_ready"], b * UNITS + p - NH + 1)
                    n, up = (P, U[p % 2][:, :]) if p < NPAIR else (F, G[p % 2][F:2 * F, :])
                    nc.vector.tensor_mul(hid[0:n, p % NH, :], act_w[0:n, p % NH, :], up).then_inc(S["hid_ready"], 1)
                    if following is not None:
                        attention_step(p, following)
                if following is not None:
                    switch(following)
                dve.wait_ge(S["down_done"], b * UNITS + UNITS)
                dve.wait_ge(S["y_free"], b * 16 + 16)
                dve.wait_ge(S["x2_moved"], b + 1)
                nc.vector.tensor_add(y[:, :], Y[:, :], x2[:, :]).then_inc(S["y_ready"], 1)
                dve.wait_ge(S["y_ready"], b + 1)
                dve.sem_inc(S["sum_free"], 1)

            with dve.Fori(0, NBLK - 1) as b:
                experts(b, b + 1)
            experts(NBLK - 1, None)

        @block.tensor
        def _(pe):
            def mm(dst, lhsT, rhs, **k):
                k.setdefault("start", True)
                k.setdefault("stop", True)
                return nc.tensor.matmul(dst, lhsT, rhs, **k)

            def attention_step(p, blk):
                if p == 0:
                    if isinstance(blk, int):
                        pe.wait_ge(S["pooled_ready"], NBLK)
                    else:
                        pe.wait_ge(S["h_in"], blk * 16)
                    mm(A2[:, :], W["q"], h_feat[:, :]).then_inc(S["q_ps"], 1)
                    wait(pe, "cwT_ready", blk)
                    mm(A0[:, :], rope_w[:, :], h_feat[:, :]).then_inc(S["rope_ps"], 1)
                    mm(A1[:, :], k_w[:, :], h_feat[:, :]).then_inc(S["k_ps"], 1)
                elif p == 5:
                    pe.wait_ge(S["rot_ready"], blk + 1)
                    pe.wait_ge(S["q_ready"], blk * NG + NG)
                    pe.wait_ge(S["krope_in"], blk * 16 + 16)
                    for t in range(TILES):
                        last = mm(A0[:, bass.ts(t, P)], h_feat[:, bass.ts(t, P)], v_w[:, :])
                    last.then_inc(S["v_ps"], 1)
                    for s in range(SPB):
                        t, r = divmod(s, SPT)
                        last = mm(A2[32 * r:32 * r + 32, bass.ts(t, SEQ)], rope_sum[0:ROPE, bass.ts(s, SEQ)],
                                  k_rope[:, bass.ts(s, SEQ)])
                    last.then_inc(S["rope_score_ps"], 1)
                elif 6 <= p < 10:
                    t = p - 6
                    if t == 0:
                        pe.wait_ge(S["rope_mask_ready"], blk + 1)
                        pe.wait_ge(S["k_ready"], blk * HG + HG)
                    elif t >= 2:
                        pe.wait_ge(S["biased_tile"], blk * TILES + t - 1)
                    for g in range(NG):
                        for r in range(SPT):
                            tok = bass.ts(t * SPT + r, SEQ)
                            last = mm((A2, A1)[t % 2][32 * r:32 * r + 32, bass.ts(g, P)], q_grp[:, g, tok], k_blk[:, :, tok])
                    last.then_inc(S["score_tile_ps"], 1)
                if 12 <= p < 16:
                    t = p - 12
                    pe.wait_ge(S["prob_tile"], blk * TILES + t + 1)
                    if t == 0:
                        pe.wait_ge(S["biased_tile"], blk * TILES + TILES)
                    else:
                        pe.wait_ge(S["probT_ready"], blk * TILES + t)
                    for g in range(NG):
                        last = nc.tensor.transpose(A1[:, bass.ts(g, P)], s_t[:, t, bass.ts(g, P)], C["ident"])
                    last.then_inc(S["probT_ps"], 1)
                if 13 <= p < 17:
                    t = p - 13
                    pe.wait_ge(S["probT_ready"], blk * TILES + t + 1)
                    if t == 0:
                        pe.wait_ge(S["v_ready"], blk * TILES + TILES)
                    elif t >= 2:
                        pe.wait_ge(S["att_ready"], blk * TILES + t - 1)
                    for g in range(NG):
                        for r in range(SPT):
                            last = mm((A0, A2)[t % 2][32 * r:32 * r + 32, bass.ts(g, HG * VC)],
                                      pt_sb[:, t % 2, g * P + 32 * r:g * P + 32 * r + 32], v_blk[:, t, r, g, :])
                    last.then_inc(S["av_ps"], 1)
                elif p == 17:
                    pe.wait_ge(S["att_ready"], blk * TILES + TILES)
                    for t in range(TILES):
                        last = nc.tensor.transpose(A1[:, bass.ts(t, P)], att[:, t, :, :].rearrange("p h d -> p (h d)"),
                                                   C["ident"])
                    last.then_inc(S["attT_ps"], 1)
                elif p == 18:
                    pe.wait_ge(S["attT_ready"], blk + 1)
                    mm(A0[:, :], W["o"], att_feat[:, :]).then_inc(S["wo_ps"], 1)
                elif p == 19:
                    pe.wait_ge(S["x2_ready"], blk + 1)
                    pe.wait_ge(S["wcat_in"], blk * (16 * SPB) + 16 * SPB)
                    for s in range(SPB):
                        t, r = divmod(s, SPT)
                        last = mm(A1[32 * r:32 * r + 32, bass.ts(t, D)], x2_next[:, bass.ts(s, SEQ)], wcat[:, s, :])
                    last.then_inc(S["c2tok_ps"], 1)
                elif p == 20:
                    pe.wait_ge(S["c2tok_ready"], blk + 1)
                    for t in range(TILES):
                        last = nc.tensor.transpose(A0[:, bass.ts(t, P)], c2_tok[:, bass.ts(t, D)], C["ident"])
                    last.then_inc(S["c2_ps"], 1)
                elif p == 21:
                    pe.wait_ge(S["c2_ready"], blk + 1)
                    for t in range(TILES):
                        last = mm(A2[:, bass.ts(t, E)], c2[:, bass.ts(t, P)], W["gate"])
                    last.then_inc(S["gate_ps"], 1)
                elif p == CWT:
                    pe.wait_ge(S["cw_ready"], blk + 1)
                    for t in range(0, TILES, 2):
                        last = nc.tensor.transpose(A0[:, bass.ts(t // 2, P)], cw[:, t:t + 2, :].rearrange("p t e -> p (t e)"),
                                                   C["ident"])
                    last.then_inc(S["cwT_ps"], 1)

            pe.wait_ge(S["consts_in"], CONSTS)
            first, width = W_COLS["k"][0], 2 * D + 2 * ROPE
            mm(A2[:, 0:width], W["kvT"], w[:, first:first + width]).then_inc(S["fold_ps"], 1)
            for j in range(2):
                pe.wait_ge(S[f"xf_in{j}"], 16 * HALF)
                for i in range(HALF):
                    for t in range(TILES):
                        last = mm(G[j][32 * t:32 * t + 32, bass.ts(i, P)], W["w1"], xf_in[HALF * j + i][:, bass.ts(t, P)])
                last.then_inc(S["hidden_ps"], 1)
            pe.wait_ge(S["dve_chain"], CHAIN_SETUP)
            for j in range(2):
                pe.wait_ge(S["tanh_done"], j + 1)
                dst = U[j][:, :].rearrange("p (i t l) -> p i t l", t=TILES, l=SEQ)
                for t in range(TILES):
                    for s in range(SPT):
                        last = mm(dst[32 * s:32 * s + 32, :, t, :], vrep[:, t, :],
                                  hidden[:, HALF * j:HALF * j + HALF, bass.ts(s, SEQ)])
                last.then_inc(S["score_ps"], 1)
            mm(Y[:, 0:NSEQ], cat_table, onehot).then_inc(S["cat_ps"], 1)
            for i in range(NBLK):
                if i % HALF == 0:
                    pe.wait_ge(S[f"xt_in{i // HALF}"], 16 * HALF)
                pe.wait_ge(S["pool_prob"], i // HALF + i + 2)
                if i >= 2:
                    pe.wait_ge(S["pooled_ready"], i - 1)
                for t in range(TILES):
                    last = mm((A0, A1)[i % 2][:, bass.ts(t, P)], xt_in[i][:, bass.ts(t, D)],
                              pool_pt[:, i % 2, t, :, :].rearrange("p s j -> p (s j)"))
                last.then_inc(S["pooled_ps"], 1)
            pe.wait_ge(S["folded"], 1)
            pe.wait_ge(S["setup"], 2)
            for p in range(UNITS):
                attention_step(p, 0)
            pe.wait_ge(S["split_lo"], NSPLIT + 1)

            def three(dst, w_hi, w_lo, m_hi, m_lo, first, final):
                mm(dst, w_hi, m_hi, start=first, stop=False)
                mm(dst, w_lo, m_hi, start=False, stop=False)
                return mm(dst, w_hi, m_lo, start=False, stop=final)

            def experts(b, following):
                pe.wait_ge(S["c_lo_ready"], b + 1)

                def down(p):
                    n = P if p < NPAIR else F
                    pe.wait_ge(S["lo_ready"], b * UNITS + p + 1)
                    if p == 0:
                        pe.wait_ge(S["sum_free"], b + 1)
                    three(Y[:, :], wd_hi[0:n, p, :], wd_lo[0:n, p, :], hid_hi[0:n, p % NH, :], hid_lo[0:n, p % NH, :],
                          p == 0, p == UNITS - 1).then_inc(S["down_done"], 1)

                for p in range(UNITS):
                    if p >= 2:
                        pe.wait_ge(S["weighted"], (b + 1) * NPAIR + p - 1)
                    three(G[p % 2][:, :], wg_hi[:, p, :], wg_lo[:, p, :], c_hi[:, :], c_lo[:, :], True, True)\
                        .then_inc(S["gate_done"], 1)
                    if p < NPAIR:
                        if p >= 2:
                            pe.wait_ge(S["hid_ready"], b * UNITS + p - 1)
                        three(U[p % 2][:, :], wu_hi[:, p, :], wu_lo[:, p, :], c_hi[:, :], c_lo[:, :], True, True)\
                            .then_inc(S["up_done"], 1)
                    if p >= NH:
                        down(p - NH)
                    if following is not None:
                        attention_step(p, following)
                for p in range(UNITS - NH, UNITS):
                    down(p)

            pe.sem_inc(S["sum_free"], 1)
            with pe.Fori(0, NBLK - 1) as b:
                experts(b, b + 1)
            experts(NBLK - 1, None)


def kernel(x, itok_B_0_2, itok_B_0_63, L0_cond_W1, L0_cond_b1, L0_cond_v, L0_attn_W_kv_down, L0_attn_W_k_up,
           L0_attn_W_v_up, L0_attn_W_q, L0_attn_W_q_rope, L0_attn_W_k_rope, L0_attn_W_o, L0_cond2_W, L0_cond2_b,
           L0_ffn_gate_w, L0_ffn_gate_bias, L0_ffn_We_gate, L0_ffn_We_up, L0_ffn_We_down, L0_ffn_Ws_gate,
           L0_ffn_Ws_up, L0_ffn_Ws_down):
    import concourse.bacc as bacc
    from concourse.bass_utils import run_bass_kernel_spmd

    def swapped(a):
        a = np.asarray(a)
        return np.concatenate([a, a[:, ROPE // 2:], a[:, :ROPE // 2]], 1)

    def experts_in(a):
        return np.ascontiguousarray(np.transpose(np.asarray(a), (1, 0, 2)).reshape(D, E * F))

    tokens = np.asarray(x).reshape(NSEQ * SEQ, D)
    arrays = {
        "x_tok": tokens.reshape(NBLK * TILES, P, D).transpose(1, 0, 2),
        "x_feat": tokens.T,
        "prompt": np.repeat(np.asarray(itok_B_0_2).reshape(NSEQ // SPT, SPT).T, SEQ, axis=0),
        "cats": np.asarray(itok_B_0_63).reshape(1, NSEQ),
        "cond_w": np.asarray(L0_cond2_W).reshape(CATS * D, D),
        "cond_b": np.asarray(L0_cond2_b),
        "weights": np.concatenate([np.asarray(a) for a in (
            np.asarray(L0_attn_W_kv_down).T, L0_attn_W_q, L0_attn_W_k_up, L0_attn_W_v_up, swapped(L0_attn_W_k_rope),
            L0_attn_W_o, swapped(L0_attn_W_q_rope), L0_cond_W1, np.tile(np.asarray(L0_cond_b1), TILES)[:, None],
            np.tile(np.asarray(L0_cond_v), TILES)[:, None], np.asarray(L0_ffn_gate_w).T)], 1),
        "consts": shape_constants(),
        "gate_bias": np.asarray(L0_ffn_gate_bias).reshape(1, E),
        "we_gate": experts_in(L0_ffn_We_gate),
        "we_up": experts_in(L0_ffn_We_up),
        "we_down": np.asarray(L0_ffn_We_down).reshape(NPAIR, 2 * F, D).transpose(1, 0, 2).reshape(2 * F, NPAIR * D),
        "ws_gu": np.concatenate([np.asarray(L0_ffn_Ws_gate), np.asarray(L0_ffn_Ws_up)], 1),
        "ws_down": np.asarray(L0_ffn_Ws_down),
    }
    nc = bacc.Bacc("TRN2", target_bir_lowering=False, num_devices=1)
    feeds, args = {}, []
    for name, a in arrays.items():
        a = np.ascontiguousarray(a)
        feeds[f"in_{name}"] = a
        args.append(nc.dram_tensor(f"in_{name}", a.shape, mybir.dt.from_np(a.dtype), kind="ExternalInput").ap())
    result = nc.dram_tensor("out_feat", (D, NSEQ * SEQ), F32, kind="ExternalOutput").ap()
    adaln_attention_moe(nc, *args, result)
    got = run_bass_kernel_spmd(nc, [feeds], core_ids=[0]).results[0]["out_feat"]
    return np.ascontiguousarray(got.T.reshape(NSEQ, SEQ, D))
```

```python
import numpy as np
import concourse.bass as bass
from concourse import mybir
from concourse.alu_op_type import AluOpType as ALU
from contextlib import ExitStack

F32 = mybir.dt.float32
F32R = mybir.dt.float32r
I32 = mybir.dt.int32
ACT = mybir.ActivationFunctionType
AX = mybir.AxisListType.X

P = 128
D = 128
SEQ = 32
NSEQ = 128
HEADS, HD = 16, 8
ROPE = 32
TOK = 512
NBLK = NSEQ * SEQ // TOK
TILES = TOK // P
SPT = P // SEQ
SPB = TOK // SEQ
CATS = 64
E, F = 64, 64
GROUPS, PER_GROUP, TOP_GROUPS, TOP_K = 8, 8, 4, 8
ROUTE_SCALE = 2.5
NPAIR = E // 2
UNITS = NPAIR + 1
ATT_SCALE = 1.0 / float(np.sqrt(HD + ROPE))
MASKED = -1.0e30
HG = 4
NG = HEADS // HG
VC = HD + 1

W_COLS, W_TOTAL = {}, 0
for _n, _w in (("kvT", D), ("q", D), ("k", D), ("v", D), ("kr", 2 * ROPE), ("o", D), ("qr", 2 * ROPE),
               ("w1", 32), ("b1", 1), ("vcol", 1), ("gate", E)):
    W_COLS[_n] = (W_TOTAL, _w)
    W_TOTAL += _w
C_COLS, C_TOTAL = {}, 0
for _n, _w in (("ident", P), ("head_of_group", HG), ("group", NG), ("causal", SEQ), ("neg0", SEQ), ("neg1", SEQ),
               ("neg2", SEQ), ("count", 3), ("rotary", SEQ), ("lower", GROUPS * GROUPS), ("index", 1)):
    C_COLS[_n] = (C_TOTAL, _w)
    C_TOTAL += _w


def shape_constants():
    c = np.zeros((P, C_TOTAL), np.float32)

    def col(name):
        a, w = C_COLS[name]
        return c[:, a:a + w]

    p = np.arange(P)
    j = (p % SEQ)[:, None]
    l = np.arange(SEQ)[None, :]
    col("ident")[:] = np.eye(P)
    col("head_of_group")[:] = (p % 32 // HD)[:, None] == np.arange(HG)
    col("group")[:] = (p // 32)[:, None] == np.arange(NG)
    col("causal")[:] = np.where(l <= j, 0.0, MASKED)
    for name, seen in (("neg0", l <= j), ("neg1", l >= j), ("neg2", l != j)):
        col(name)[:] = np.where(seen, 0.0, MASKED)
        col("count")[:, int(name[-1])] = seen.sum(1)
    inv = (1.0 / np.float32(10000.0) ** (np.arange(0, ROPE, 2, dtype=np.float32) / ROPE)).astype(np.float32)
    angle = np.outer(inv, np.arange(SEQ, dtype=np.float32)).astype(np.float32)
    half = p % ROPE % (ROPE // 2)
    sign = np.where(p % ROPE < ROPE // 2, -1.0, 1.0)[:, None]
    col("rotary")[:] = np.where((p < 2 * ROPE)[:, None], np.cos(angle)[half], np.sin(angle)[half] * sign)
    g = np.arange(GROUPS)
    col("lower")[:] = (g[None, :] < g[:, None]).reshape(1, -1)
    col("index")[:, 0] = p
    return c


def adaln_attention_moe(nc, x_tok, x_feat, prompt, cats, cond_w, cond_b, weights, consts, gate_bias,
                        we_gate, we_up, we_down, ws_gu, ws_down, out):
    ctx = ExitStack()
    with ctx:
        def sb(name, shape, dt=F32):
            return ctx.enter_context(nc.sbuf_tensor(name, shape, dt))

        def sem(name):
            return ctx.enter_context(nc.semaphore(name))

        w = sb("w", [P, W_TOTAL])
        c = sb("c", [P, C_TOTAL])
        W = {n: w[:, a:a + k] for n, (a, k) in W_COLS.items()}
        C = {n: c[:, a:a + k] for n, (a, k) in C_COLS.items()}
        wg_hi, wg_lo = sb("wg_hi", [P, UNITS, P], F32R), sb("wg_lo", [P, UNITS, P], F32R)
        wu_hi, wu_lo = sb("wu_hi", [P, NPAIR, P], F32R), sb("wu_lo", [P, NPAIR, P], F32R)
        wd_hi, wd_lo = sb("wd_hi", [P, UNITS, D], F32R), sb("wd_lo", [P, UNITS, D], F32R)
        k_w, v_w = sb("k_w", [P, D]), sb("v_w", [P, D])
        rope_w = sb("rope_w", [P, P])
        vrep = sb("vrep", [P, TILES, SEQ])
        gbias = sb("gbias", [P, E])
        cat_row = sb("cat_row", [CATS, NSEQ], I32)
        cat_bias = sb("cat_bias", [P, NSEQ])

        xf = sb("xf", [P, TOK])
        s_t = sb("s_t", [P, TILES, HEADS * SEQ])
        small = sb("small", [P, 16])
        h_feat = sb("h_feat", [P, TOK])
        q_grp = sb("q_grp", [P, NG, TOK])
        k_blk = sb("k_blk", [P, HG, TOK])
        wcat = k_blk[:, :, :].rearrange("p a b -> p (a b)").rearrange("p (s h) -> p s h", h=D)
        v_blk = sb("v_blk", [P, TILES, SPT, NG, HG * VC])
        pt_sb = sb("pt_sb", [P, 2, NG * P])
        rot = pt_sb[0:2 * ROPE]
        rope_sum = sb("rope_sum", [2 * ROPE, TOK])
        k_rope = sb("k_rope", [ROPE, TOK])
        rope_mask = sb("rope_mask", [P, TILES, SEQ])
        head_max = sb("head_max", [P, TILES, HEADS])
        rden = sb("rden", [P, TILES, HEADS])
        att = sb("att", [P, TILES, HEADS, HD])
        att_feat = h_feat
        x2_next = sb("x2_next", [P, TOK])
        c2_tok = att[:, :, :, :].rearrange("p t h d -> p (t h d)")
        c2 = sb("c2", [P, TOK])
        score = sb("score", [P, TILES, E])
        biased = sb("biased", [P, TILES, E])
        rt = sb("rt", [P, 3, TILES * E])
        best = sb("best", [P, TILES, 8])
        cw = sb("cw", [P, TILES, E])
        cw_feat = sb("cw_feat", [2 * E, TOK // 2])

        c_hi, c_lo = sb("c_hi", [P, TOK], F32R), sb("c_lo", [P, TOK], F32R)
        x2 = sb("x2", [P, TOK])
        NCW = 4
        NH = 3
        cwb = sb("cwb", [P, NCW, TOK])
        act_w = sb("act_w", [P, NH, TOK])
        hid = sb("hid", [P, NH, TOK])
        hid_hi, hid_lo = sb("hid_hi", [P, NH, TOK], F32R), sb("hid_lo", [P, NH, TOK], F32R)
        y = sb("y", [P, TOK])

        stage = cwb
        xf_in = [k_blk[:, i, :] for i in range(4)] + [xf[:, :], x2_next[:, :], c2_tok, h_feat[:, :]]
        xt_in = [q_grp[:, i, :] for i in range(4)] + [act_w[:, 2, :], hid[:, 2, :], y[:, :],
                                                      rt[:, 0:2, :].rearrange("p a n -> p (a n)")]
        hidden = s_t[:, 0:2, :].rearrange("p a n -> p (a n)").rearrange("p (i n) -> p i n", n=P)
        pooled = s_t[:, 2:4, :]
        pool_pt = pt_sb[:, :, :].rearrange("p i (t s j) -> p i t s j", t=TILES, s=SPT)
        tiles32 = "p a (n l) -> p (a n) l"
        neg = act_w[:, 0:2, :].rearrange(tiles32, l=SEQ)
        pool_p = hid[:, 0:2, :].rearrange(tiles32, l=SEQ)
        mask_tmp = hid[:, 0:2, :].rearrange(tiles32, l=SEQ)
        stats = x2[:, 0:8 * NSEQ // SPT].rearrange("p (k n) -> p k n", k=8)
        pt_i = best[:, :, :].rearrange("p a n -> p (a n)")[:, 0:NSEQ // SPT].bitcast(I32)
        cat_table = c2[0:CATS, 0:D]
        onehot = c2[0:CATS, D:D + NSEQ]

        h_dram = nc.dram_tensor("pooled_scratch", [P, (NBLK + 1) * TOK], F32).ap()
        cw_dram = nc.dram_tensor("cw_scratch", [E, NSEQ * SEQ], F32).ap()

        def bank(name):
            return ctx.enter_context(nc.psum_tensor(name, [P, 512], F32))

        A0, A1, A2 = bank("A0"), bank("A1"), bank("A2")
        G = [bank("G0"), bank("G1")]
        U = [bank("U0"), bank("U1")]
        Y = bank("Y")

        S = {}
        for name in """consts_in xf_in0 xf_in1 xt_ps xt_ready stage_in0 stage_in1 stage_in2 stage_in3
                small_in split_hi split_lo setup fold_ps folded cat_ps cat_read hidden_ps tanh_done score_ps pool_sub pool_exp
                pool_prob pooled_ps pooled_ready h_stored0 h_stored1
                h_in res_in krope_in krope_ready wcat_in cw_stored y_free cwb_in0 cwb_in1 cwb_in2 cwb_in3
                q_ps rope_ps k_ps q_ready rot_ready rope_summed k_ready v_ps v_ready rope_score_ps rope_mask_ready
                score_tile_ps biased_tile sub_tile prob_tile probT_ps probT_ready av_ps att_ready attT_ps attT_ready
                wo_ps x2_ready c2tok_ps c2tok_ready c2_ps c2_ready gate_ps tanh_gate score_ready biased_ready cw_ready cwT_ps cwT_ready
                dve_chain c_hi_ready c_lo_ready x2_moved gate_done silu_done up_done weighted hid_ready hi_ready
                lo_ready shared_lo_ready down_done y_ready sum_free""".split():
            S[name] = sem(name)
        stage_in = [S[f"stage_in{i}"] for i in range(4)]
        cwb_in = [S[f"cwb_in{i}"] for i in range(4)]

        EXPS = 10
        LENT = EXPS + 1

        def gate_bank(p):
            return A0 if p == LENT else G[p % 2]

        def up_bank(p):
            return A2 if p == LENT else U[p % 2]

        def wait(eng, name, value):
            if not (isinstance(value, int) and value <= 0):
                eng.wait_ge(S[name], value)

        HALF = NBLK // 2
        CONSTS = 6 * 16
        NSPLIT = 24
        EARLY = 6
        SPLITS = {}
        for _i, _p in enumerate([4, 4, 5, 6, 7, 8, 9, 9, 11, 12, 14, 16, 20, 21, 21, 22, 22, 23, 23]):
            SPLITS.setdefault(_p, []).append(EARLY + _i)
        LATER = 16
        assert EARLY + _i == NSPLIT
        CHAIN_SETUP = 13
        CHAIN_POOL = 10
        CHAIN_BASE = CHAIN_SETUP + CHAIN_POOL
        CHAIN = 25
        CWT = 31
        WARM_LOADS, WARM_SOFTMAX, WARM_POOLED = 5, 16, 4
        WARM = {0: 10, 5: 4, 9: 12, 12: 3, 13: 3, 14: 3, 15: 3, 16: 3, 17: 3, 18: 4, 19: 3, 20: 3, 21: 34}
        block = ctx.enter_context(nc.Block())

        @block.sync
        def _(sp):
            for dst, src in ((c[:, :], consts), (w[:, :], weights), (pt_i, prompt),
                             (cat_row[:, :], cats.to_broadcast([CATS, NSEQ])), (cat_table, cond_b),
                             (gbias[:, :], gate_bias.to_broadcast([P, E]))):
                sp.dma_start(dst, src).then_inc(S["consts_in"], 16)

            def stage_load(i):
                if i >= 4:
                    sp.wait_ge(S["split_lo"], i - 3)
                if i < NSPLIT:
                    src = (we_gate, we_up, we_down)[i // 8][:, bass.ts(i % 8, TOK)]
                    sp.dma_start(stage[:, i % 4, :], src).then_inc(stage_in[i % 4], 16)
                else:
                    sp.dma_start(stage[:, 0, 0:2 * F], ws_gu).then_inc(stage_in[0], 16)
                    sp.dma_start(stage[0:F, 0, 2 * F:2 * F + D], ws_down).then_inc(S["small_in"], 16)

            kinds = []

            def attention_loads(p, blk):
                if p == 0:
                    wait(sp, "x2_ready", blk)
                    sp.dma_start(xf[:, :], x_feat[:, bass.ds(blk * TOK, TOK)]).then_inc(S["res_in"], 16)
                elif p == 4:
                    sp.wait_ge(S["rope_summed"], blk + 1)
                    sp.dma_start(k_rope[:, :], rope_sum[ROPE:2 * ROPE, :]).then_inc(S["krope_in"], 16)
                elif 9 <= p < 13:
                    if p == 9:
                        kinds.clear()
                    for s in range(4 * (p - 9), 4 * (p - 9) + 4):
                        kinds.append(sp.value_load(cat_row[0:1, bass.ds(blk * SPB + s, 1)], min_val=0, max_val=CATS - 1))
                elif 13 <= p < 17:
                    if p == 13:
                        sp.wait_ge(S["score_tile_ps"], blk * TILES + TILES)
                    for s in range(4 * (p - 13), 4 * (p - 13) + 4):
                        sp.dma_start(wcat[:, s, :], cond_w[bass.ds(kinds[s] * D, D), :]).then_inc(S["wcat_in"], 16)
                elif p == 21:
                    sp.wait_ge(S["wo_ps"], blk + 1)
                    sp.dma_start(h_feat[:, :], h_dram[:, bass.ds(blk * TOK + TOK, TOK)]).then_inc(S["h_in"], 16)
                elif p == 32:
                    sp.wait_ge(S["cwT_ready"], blk + 1)
                    dst = cw_dram[:, bass.ds(blk * TOK, TOK)].rearrange("e (u two n) -> e u two n", two=2, n=P)
                    for i in range(2):
                        sp.dma_start(dst[:, :, i, :], cw_feat[E * i:E * i + E, :].rearrange("e (u n) -> e u n", n=P))\
                            .then_inc(S["cw_stored"], 16)

            for j in range(2):
                for i in range(HALF * j, HALF * j + HALF):
                    sp.dma_start(xf_in[i], x_feat[:, bass.ts(i, TOK)]).then_inc(S[f"xf_in{j}"], 16)
            for i in range(4):
                stage_load(i)
            for i in range(1, NBLK):
                sp.wait_ge(S["pooled_ready"], i + 1)
                sp.dma_start(h_dram[:, bass.ts(i, TOK)], pooled[:, i % 2, :]).then_inc(S[f"h_stored{i % 2}"], 16)
                if i >= 2:
                    stage_load(i + 2)
            sp.dma_start(h_dram[:, bass.ts(NBLK, TOK)], pooled[:, 1, :]).then_inc(S["h_stored0"], 16)
            attention_loads(0, 0)
            for p in range(9, 13):
                attention_loads(p, 0)
            for i in range(NBLK + 2, 18):
                stage_load(i)
            for p in range(13, 17):
                attention_loads(p, 0)
            for i in range(2):
                sp.wait_ge(S[f"h_stored{i}"], 16 * HALF)
            attention_loads(21, 0)
            for i in range(18, NSPLIT + 1):
                stage_load(i)
            attention_loads(32, 0)

            def experts_loads(b, following):
                for p in range(UNITS):
                    if following is not None:
                        attention_loads(p, following)
                    if p < NPAIR:
                        sp.wait_ge(S["weighted"], (b + 1) * NPAIR + max(0, p - NCW + 1))
                        if p == 0:
                            sp.wait_ge(S["split_lo"], NSPLIT + 1)
                            sp.wait_ge(S["cw_stored"], (b + 1) * 32)
                        src = cw_dram[2 * p:2 * p + 2, bass.ds(b * TOK, TOK)].unsqueeze(1).to_broadcast([2, F, TOK])
                        sp.dma_start(cwb[:, p % NCW, :], src).then_inc(cwb_in[p % NCW], 16)

            with sp.Fori(0, NBLK - 1) as b:
                experts_loads(b, b + 1)
            experts_loads(NBLK - 1, None)
            sp.wait_ge(S["h_in"], 16 * NBLK)
            sp.wait_ge(S["y_free"], 16 * NBLK + 16)

        @block.scalar
        def _(act):
            def attention_step(p, blk):
                if 1 <= p < 5:
                    if p == 1:
                        act.wait_ge(S["q_ps"], blk + 1)
                    nc.scalar.mul(q_grp[:, p - 1, :], A2[:, :], C["group"][:, p - 1:p]).then_inc(S["q_ready"], 1)
                elif 5 <= p < 9:
                    s = p - 5
                    if s == 0:
                        act.wait_ge(S["v_ps"], blk + 1)
                    for r in range(HG):
                        src = A0[32 * s:32 * s + 32, :].rearrange("p (t c r d) -> p t c r d", t=TILES, c=NG, r=HG)
                        dst = v_blk[32 * r:32 * r + 32, :, s, :, r * VC:r * VC + HD]
                        last = nc.scalar.copy(dst, src[:, :, :, r, :])
                    last.then_inc(S["v_ready"], 1)
                elif p == EXPS:
                    for t in range(TILES):
                        act.wait_ge(S["sub_tile"], blk * TILES + t + 1)
                        nc.scalar.activation(s_t[:, t, :], s_t[:, t, :], ACT.Exp, scale=ATT_SCALE)\
                            .then_inc(S["prob_tile"], 1)
                        if t == 2 and not isinstance(blk, int):
                            rounded(blk - 1, p)
                elif 12 <= p < 16:
                    t = p - 12
                    act.wait_ge(S["probT_ps"], blk * TILES + t + 1)
                    if t >= 2:
                        act.wait_ge(S["av_ps"], blk * TILES + t - 1)
                    nc.scalar.copy(pt_sb[:, t % 2, :], A1[:, :]).then_inc(S["probT_ready"], 1)
                elif p == 17:
                    act.wait_ge(S["attT_ps"], blk + 1)
                    nc.scalar.copy(att_feat[:, :], A1[:, :]).then_inc(S["attT_ready"], 1)
                elif p == 19:
                    act.wait_ge(S["c2tok_ps"], blk + 1)
                    nc.scalar.copy(c2_tok, A1[:, :]).then_inc(S["c2tok_ready"], 1)
                elif p == 21:
                    act.wait_ge(S["gate_ps"], blk + 1)
                    nc.scalar.activation(score[:, :, :].rearrange("p t e -> p (t e)"), A2[:, 0:TILES * E], ACT.Tanh,
                                         scale=0.5).then_inc(S["tanh_gate"], 1)
                    act.wait_ge(S["tanh_gate"], blk + 1)
                    nc.scalar.activation(score[:, :, :].rearrange("p t e -> p (t e)"),
                                         score[:, :, :].rearrange("p t e -> p (t e)"), ACT.Copy, bias=0.5,
                                         scale=0.5).then_inc(S["score_ready"], 1)
                elif p == CWT:
                    act.wait_ge(S["cwT_ps"], blk + 1)
                    wait(act, "cw_stored", blk * 32)
                    nc.scalar.copy(cw_feat[:, :], A0[:, 0:TOK // 2]).then_inc(S["cwT_ready"], 1)

            def switch(blk):
                wait(act, "gate_done", blk * UNITS)
                act.wait_ge(S["c2_ready"], blk + 1)
                nc.scalar.copy(c_hi[:, :], c2[:, :]).then_inc(S["c_hi_ready"], 1)

            def split(i):
                act.wait_ge(stage_in[i % 4], 16 * (i // 4 + 1))
                if i < NSPLIT:
                    hi = (wg_hi, wu_hi, wd_hi)[i // 8]
                    nc.scalar.copy(hi[:, 4 * (i % 8):4 * (i % 8) + 4, :].rearrange("p a b -> p (a b)"),
                                   stage[:, i % 4, :]).then_inc(S["split_hi"], 1)
                else:
                    act.wait_ge(S["small_in"], 16)
                    nc.scalar.copy(wg_hi[:, NPAIR, :], stage[:, 0, 0:2 * F])
                    nc.scalar.copy(wd_hi[0:F, NPAIR, :], stage[0:F, 0, 2 * F:2 * F + D]).then_inc(S["split_hi"], 1)

            act.sem_inc(S["y_free"], 16)
            act.wait_ge(S["consts_in"], CONSTS)
            act.wait_ge(S["fold_ps"], 1)
            nc.scalar.copy(k_w[:, :], A2[:, 0:D])
            nc.scalar.copy(v_w[:, :], A2[:, D:2 * D])
            for i in range(2):
                nc.scalar.copy(rope_w[:, 2 * ROPE * i:2 * ROPE * i + ROPE], W["qr"][:, bass.ts(i, ROPE)])
                last = nc.scalar.copy(rope_w[:, 2 * ROPE * i + ROPE:2 * ROPE * (i + 1)],
                                      A2[:, 2 * D + ROPE * i:2 * D + ROPE * (i + 1)])
            last.then_inc(S["folded"], 1)
            def pool_hidden(j):
                act.wait_ge(S["hidden_ps"], j + 1)
                nc.scalar.activation(hidden[:, HALF * j:HALF * j + HALF, :].rearrange("p i n -> p (i n)"), G[j][:, :],
                                     ACT.Tanh, bias=W["b1"]).then_inc(S["tanh_done"], 1)

            def turned(i):
                act.wait_ge(S["xt_ps"], i + 1)
                nc.scalar.copy(xt_in[i], (A0, A1)[i % 2][:, :]).then_inc(S["xt_ready"], 1)

            def pool_exp(j):
                act.wait_ge(S["pool_sub"], j + 1)
                part = pool_p[:, HALF * TILES * j:HALF * TILES * (j + 1), :]
                nc.scalar.activation(part, part, ACT.Exp).then_inc(S["pool_exp"], 1)

            pool_hidden(0)
            for i in range(HALF):
                turned(i)
            pool_hidden(1)
            for i in range(HALF, HALF + 2):
                turned(i)
            pool_exp(0)
            for i in range(HALF + 2, NBLK):
                turned(i)
            pool_exp(1)
            act.wait_ge(S["cat_ps"], 1)
            nc.scalar.copy(cat_bias[:, :], Y[:, 0:NSEQ]).then_inc(S["cat_read"], 1)
            for i in range(NBLK):
                act.wait_ge(S["pooled_ps"], i + 1)
                if i == 0:
                    nc.scalar.copy(h_feat[:, :], A0[:, :]).then_inc(S["pooled_ready"], 1)
                    split(0)
                    continue
                if i >= 3:
                    act.wait_ge(S[f"h_stored{i % 2}"], 16 * ((i - 1) // 2))
                nc.scalar.copy(pooled[:, i % 2, :], (A0, A1)[i % 2][:, :]).then_inc(S["pooled_ready"], 1)
                if i < EARLY:
                    split(i)
            for p in range(UNITS):
                attention_step(p, 0)
                if p == 21:
                    switch(0)
                for i in SPLITS.get(p, ()):
                    split(i)

            def silu(b, p):
                act.wait_ge(S["gate_done"], b * UNITS + p + 1)
                if p < NPAIR:
                    nc.scalar.activation(gate_bank(p)[:, :], gate_bank(p)[:, :], ACT.Silu).then_inc(S["silu_done"], 1)
                else:
                    act.wait_ge(S["hid_ready"], b * UNITS + p - NH + 1)
                    nc.scalar.activation(act_w[0:F, p % NH, :], gate_bank(p)[0:F, :], ACT.Silu)\
                        .then_inc(S["silu_done"], 1)

            def rounded(b, p):
                act.wait_ge(S["hid_ready"], b * UNITS + p + 1)
                n = P if p < NPAIR else F
                nc.scalar.copy(hid_hi[0:n, p % NH, :], hid[0:n, p % NH, :]).then_inc(S["hi_ready"], 1)

            def experts(b, following):
                for p in range(1, UNITS):
                    if p < NPAIR:
                        silu(b, p)
                        if p == EXPS + 2 and following is not None:
                            attention_step(p, following)
                            rounded(b, p - 1)
                            continue
                        if p != EXPS + 1 or following is None:
                            rounded(b, p - 1)
                    else:
                        rounded(b, p - 1)
                        silu(b, p)
                    if following is not None:
                        attention_step(p, following)
                    if p == 4:
                        nc.scalar.copy(x2[:, :], x2_next[:, :]).then_inc(S["x2_moved"], 1)
                rounded(b, UNITS - 1)
                if following is not None:
                    switch(following)
                    silu(following, 0)
                act.wait_ge(S["y_ready"], b + 1)
                act.dma_start(out[:, bass.ds(b * TOK, TOK)], y[:, :]).then_inc(S["y_free"], 16)

            silu(0, 0)
            with act.Fori(0, NBLK - 1) as b:
                experts(b, b + 1)
            experts(NBLK - 1, None)

        @block.gpsimd
        def _(pool):
            def rope_add(blk):
                pool.wait_ge(S["rot_ready"], blk + 1)
                nc.gpsimd.tensor_add(rope_sum[:, :], rot[:, 0, :], rot[:, 1, :]).then_inc(S["rope_summed"], 1)

            def attention_step(p, blk):
                if 6 <= p < 10:
                    t = p - 6
                    pool.wait_ge(S["biased_tile"], blk * TILES + t + 1)
                    s = s_t[:, t, :].rearrange("p (h k) -> p h k", k=SEQ)
                    nc.gpsimd.tensor_sub(s, s, head_max[:, t, :].unsqueeze(2).to_broadcast([P, HEADS, SEQ]))\
                        .then_inc(S["sub_tile"], 1)
                elif p == 20:
                    pool.wait_ge(S["score_ready"], blk + 1)
                    nc.gpsimd.tensor_add(biased[:, :, :], score[:, :, :],
                                         gbias[:, :].unsqueeze(1).to_broadcast([P, TILES, E])).then_inc(S["biased_ready"], 1)

            def split(i):
                pool.wait_ge(S["split_hi"], i + 1)
                if i < NSPLIT:
                    hi, lo = ((wg_hi, wg_lo), (wu_hi, wu_lo), (wd_hi, wd_lo))[i // 8]
                    hi, lo = (a[:, 4 * (i % 8):4 * (i % 8) + 4, :].rearrange("p a b -> p (a b)") for a in (hi, lo))
                    nc.gpsimd.tensor_sub(lo, stage[:, i % 4, :], hi.bitcast(F32)).then_inc(S["split_lo"], 1)
                else:
                    nc.gpsimd.tensor_sub(wg_lo[:, NPAIR, :], stage[:, 0, 0:2 * F], wg_hi[:, NPAIR, :].bitcast(F32))
                    nc.gpsimd.tensor_sub(wd_lo[0:F, NPAIR, :], stage[0:F, 0, 2 * F:2 * F + D],
                                         wd_hi[0:F, NPAIR, :].bitcast(F32)).then_inc(S["split_lo"], 1)

            pool.memset(pool_pt[:, :, :, :, :], 0.0)
            nc.gpsimd.memset(v_blk[:, :, :, :, :], 0.0).then_inc(S["setup"], 1)
            pool.wait_ge(S["setup"], 1)
            v_ones = v_blk[:, :, :, :, :].rearrange("p t s c m -> p (t s c) m")
            for r in range(HG):
                last = nc.gpsimd.memset(v_ones[32 * r:32 * r + 32, :, r * VC + HD:r * VC + VC], 1.0)
            last.then_inc(S["setup"], 1)
            pool.wait_ge(S["setup"], 2)
            for i in range(EARLY):
                split(i)
            rope_add(0)
            for p in range(UNITS):
                attention_step(p, 0)
                for i in SPLITS.get(p, ()):
                    split(i)
            rope_add(1)

            def experts(b, following):
                for p in range(UNITS):
                    if p < NPAIR:
                        pool.wait_ge(S["hi_ready"], b * UNITS + p + 1)
                        nc.gpsimd.tensor_sub(hid_lo[:, p % NH, :], hid[:, p % NH, :],
                                             hid_hi[:, p % NH, :].bitcast(F32)).then_inc(S["lo_ready"], 1)
                    if following is not None:
                        attention_step(p, following)
                if following is not None:
                    rope_add(following + 1)

            with pool.Fori(0, NBLK - 1) as b:
                experts(b, b + 1)
            experts(NBLK - 1, None)

        @block.vector
        def _(dve):
            steps = [0]

            def chain(ins, blk):
                steps[0] += 1
                ins.then_inc(S["dve_chain"], 1)
                dve.wait_ge(S["dve_chain"], CHAIN_BASE + blk * CHAIN + steps[0])

            def rotate(blk):
                dve.wait_ge(S["rope_ps"], blk + 1)
                for i in range(2):
                    rows = slice(2 * ROPE * i, 2 * ROPE * (i + 1))
                    last = nc.vector.tensor_mul(
                        rot[:, i, :].rearrange("p (s t) -> p s t", t=SEQ),
                        A0[rows, :].rearrange("p (s t) -> p s t", t=SEQ),
                        C["rotary"][rows].unsqueeze(1).to_broadcast([2 * ROPE, SPB, SEQ]))
                last.then_inc(S["rot_ready"], 1)

            def after_chain(blk):
                dve.wait_ge(S["dve_chain"], CHAIN_BASE + blk * CHAIN + steps[0])

            def attention_step(p, blk):
                if p == 0:
                    steps[0] = 0
                elif 1 <= p < 5:
                    if p == 2 and isinstance(blk, int):
                        dve.wait_ge(S["rope_summed"], 1)
                        nc.vector.tensor_copy(k_rope[:, :], rope_sum[ROPE:2 * ROPE, :]).then_inc(S["krope_ready"], 1)
                    h = p - 1
                    if h == 0:
                        dve.wait_ge(S["k_ps"], blk + 1)
                    nc.vector.tensor_scalar(k_blk[:, h, :], A1[:, :], C["head_of_group"][:, h:h + 1], None, ALU.mult)\
                        .then_inc(S["k_ready"], 1)
                elif p == 5:
                    dve.wait_ge(S["rope_score_ps"], blk + 1)
                    nc.vector.tensor_add(rope_mask[:, :, :], A2[:, 0:TILES * SEQ].rearrange("p (t k) -> p t k", k=SEQ),
                                         C["causal"].unsqueeze(1).to_broadcast([P, TILES, SEQ]))\
                        .then_inc(S["rope_mask_ready"], 1)
                elif 6 <= p < 10:
                    t = p - 6
                    if t == 0:
                        dve.wait_ge(S["rope_mask_ready"], blk + 1)
                    dve.wait_ge(S["score_tile_ps"], blk * TILES + t + 1)
                    s = s_t[:, t, :].rearrange("p (h k) -> p h k", k=SEQ)
                    chain(nc.vector.tensor_add(s, (A2, A1)[t % 2][:, :].rearrange("p (h k) -> p h k", k=SEQ),
                                               rope_mask[:, t, :].unsqueeze(1).to_broadcast([P, HEADS, SEQ])), blk)
                    nc.vector.tensor_reduce(head_max[:, t, :], s, AX, ALU.max).then_inc(S["biased_tile"], 1)
                elif 13 <= p < 17:
                    t = p - 13
                    ps = (A0, A2)[t % 2][:, 0:HEADS * VC].rearrange("p (h m) -> p h m", m=VC)
                    dve.wait_ge(S["av_ps"], blk * TILES + t + 1)
                    chain(nc.vector.reciprocal(rden[:, t, :], ps[:, :, HD]), blk)
                    nc.vector.tensor_mul(att[:, t, :, :], ps[:, :, 0:HD],
                                         rden[:, t, :].unsqueeze(2).to_broadcast([P, HEADS, HD]))\
                        .then_inc(S["att_ready"], 1)
                elif p == 18:
                    wait(dve, "x2_moved", blk)
                    dve.wait_ge(S["res_in"], 16 * blk + 16)
                    dve.wait_ge(S["wo_ps"], blk + 1)
                    nc.vector.tensor_add(x2_next[:, :], A0[:, :], xf[:, :]).then_inc(S["x2_ready"], 1)
                elif p == 20:
                    dve.wait_ge(S["c2_ps"], blk + 1)
                    nc.vector.tensor_add(c2[:, :].rearrange("p (s t) -> p s t", t=SEQ),
                                         A0[:, :].rearrange("p (s t) -> p s t", t=SEQ),
                                         cat_bias[:, bass.ds(blk * SPB, SPB)].unsqueeze(2).to_broadcast([P, SPB, SEQ]))\
                        .then_inc(S["c2_ready"], 1)
                elif 22 <= p < 30:
                    routing(2 * (p - 22), blk)

            def attention_half_step(p, blk):
                if 23 <= p < 31:
                    routing(2 * (p - 23) + 1, blk)

            flat = biased[:, :, :].rearrange("p t (g e) -> p (t g) e", e=PER_GROUP)
            TG = TILES * GROUPS
            rest = rt[:, 0, :].rearrange("p (t e) -> p t e", e=E)
            TAKEN, NO_SCORE = -3.0e38, 3.0e38

            def sorted_pair(level, which):
                width, at = PER_GROUP >> (level + 1), TG * (PER_GROUP - (PER_GROUP >> level))
                return rt[:, which, at:at + TG * width].rearrange("p (n w) -> p n w", w=width)

            def merge(level):
                width = PER_GROUP >> (level + 1)
                v, low = sorted_pair(level - 1, 0), sorted_pair(level - 1, 1)
                nc.vector.tensor_tensor(sorted_pair(level, 0), v[:, :, 0:width], v[:, :, width:2 * width], ALU.max)
                nc.vector.tensor_tensor(sorted_pair(level, 1), v[:, :, 0:width], v[:, :, width:2 * width], ALU.min)
                return nc.vector.tensor_tensor(others(level), low[:, :, 0:width], low[:, :, width:2 * width], ALU.max)

            def others(level):
                width = PER_GROUP >> (level + 1)
                return rt[:, 2, 0:TG * width].rearrange("p (n w) -> p n w", w=width)

            def routing(step, blk):
                if step not in (0, 6, 8, 11, 12):
                    after_chain(blk)
                group_score, group_left = rt[:, 2, 64:64 + TG], rt[:, 2, 128:128 + TG]
                if step == 0:
                    dve.wait_ge(S["biased_ready"], blk + 1)
                    a, b = flat[:, :, 0:PER_GROUP // 2], flat[:, :, PER_GROUP // 2:PER_GROUP]
                    nc.vector.tensor_tensor(sorted_pair(0, 0), a, b, ALU.max)
                    last = nc.vector.tensor_tensor(sorted_pair(0, 1), a, b, ALU.min)
                elif step in (1, 3):
                    last = merge((step + 1) // 2)
                elif step in (2, 4):
                    low = sorted_pair(step // 2, 1)
                    last = nc.vector.tensor_tensor(low, low, others(step // 2), ALU.max)
                elif step == 5:
                    last = nc.vector.tensor_add(group_score, sorted_pair(2, 0)[:, :, 0], sorted_pair(2, 1)[:, :, 0])
                elif step == 6:
                    for t in range(TILES):
                        last = nc.vector.max(best[:, t, :], group_score[:, bass.ts(t, GROUPS)])
                elif step == 7:
                    last = nc.vector.memset(best[:, :, TOP_GROUPS:], NO_SCORE)
                elif step == 8:
                    for t in range(TILES):
                        part = bass.ts(t, GROUPS)
                        last = nc.vector.match_replace(group_left[:, part], best[:, t, :], group_score[:, part], TAKEN)
                elif step == 9:
                    last = nc.vector.tensor_scalar(group_left, group_left, TAKEN, MASKED, ALU.not_equal, ALU.mult)
                elif step == 10:
                    last = nc.vector.tensor_add(flat, flat, group_left.unsqueeze(2).to_broadcast([P, TG, PER_GROUP]))
                elif step == 11:
                    for t in range(TILES):
                        last = nc.vector.max(best[:, t, :], biased[:, t, :])
                elif step == 12:
                    for t in range(TILES):
                        last = nc.vector.match_replace(rest[:, t, :], best[:, t, :], biased[:, t, :], TAKEN)
                elif step == 13:
                    last = nc.vector.scalar_tensor_tensor(rt[:, 0, :], rt[:, 0, :], TAKEN,
                                                          score[:, :, :].rearrange("p t e -> p (t e)"),
                                                          ALU.is_equal, ALU.mult)
                elif step == 14:
                    last = nc.vector.tensor_reduce(small[:, 0:TILES], rest, AX, ALU.add)
                elif step == 15:
                    chain(nc.vector.tensor_scalar(small[:, 0:TILES], small[:, 0:TILES], 1e-20, 1.0 / ROUTE_SCALE,
                                                  ALU.add, ALU.mult), blk)
                    chain(nc.vector.reciprocal(small[:, 4:4 + TILES], small[:, 0:TILES]), blk)
                    nc.vector.tensor_mul(cw[:, :, :], rest, small[:, 4:4 + TILES].unsqueeze(2)
                                         .to_broadcast([P, TILES, E])).then_inc(S["cw_ready"], 1)
                    assert steps[0] == CHAIN, steps[0]
                    return
                steps[0] += 1
                last.then_inc(S["dve_chain"], 1)
                if step + 1 in (6, 8, 11, 12):
                    after_chain(blk)

            def setup(ins):
                steps[0] += 1
                ins.then_inc(S["dve_chain"], 1)
                dve.wait_ge(S["dve_chain"], steps[0])

            dve.sem_inc(S["weighted"], NPAIR)
            nc.vector.memset(vrep[:, :, :], 0.0)
            dve.wait_ge(S["consts_in"], CONSTS)
            kind, is_kind, count = stats[:, 0, :], [stats[:, 1 + k, :] for k in range(3)], [stats[:, 4 + k, :] for k in range(2)]
            setup(nc.vector.tensor_copy(kind, pt_i))
            setup(nc.vector.tensor_copy(onehot, cat_row[:, :]))
            for t in range(TILES):
                rows = slice(SEQ * t, SEQ * t + SEQ)
                nc.vector.tensor_copy(vrep[rows, t, :], W["vcol"][rows].to_broadcast([SEQ, SEQ]))
            setup(nc.vector.tensor_scalar(onehot, onehot, C["index"][0:CATS], None, ALU.is_equal))
            setup(nc.vector.tensor_scalar(is_kind[0], kind, 0.0, None, ALU.is_equal))
            setup(nc.vector.tensor_scalar(is_kind[1], kind, 1.0, None, ALU.is_equal))
            setup(nc.vector.tensor_add(is_kind[2], is_kind[0], is_kind[1]))
            setup(nc.vector.tensor_scalar(is_kind[2], is_kind[2], -1.0, 1.0, ALU.mult, ALU.add))
            wide = [P, NSEQ // SPT, SEQ]
            for k in range(3):
                mask = C[f"neg{k}"].unsqueeze(1).to_broadcast(wide)
                setup(nc.vector.tensor_mul(neg if k == 0 else mask_tmp, mask, is_kind[k].unsqueeze(2).to_broadcast(wide)))
                if k:
                    nc.vector.tensor_add(neg, neg, mask_tmp)
                    setup(nc.vector.scalar_tensor_tensor(count[k % 2], is_kind[k], C["count"][:, k:k + 1],
                                                         count[(k + 1) % 2], ALU.mult, ALU.add))
                else:
                    setup(nc.vector.tensor_scalar(count[0], is_kind[0], C["count"][:, 0:1], None, ALU.mult))
            assert steps[0] == CHAIN_SETUP, steps[0]

            largest, total = stats[:, 6, :], stats[:, 7, :]

            def half(a, j):
                return a[:, HALF * TILES * j:HALF * TILES * (j + 1)]

            def over_row(a):
                return a.unsqueeze(2).to_broadcast([P, HALF * TILES, SEQ])

            for j in range(2):
                part = half(pool_p, j)
                dve.wait_ge(S["score_ps"], j + 1)
                setup(nc.vector.tensor_add(part, U[j][:, :].rearrange("p (n l) -> p n l", l=SEQ), half(neg, j)))
                setup(nc.vector.tensor_reduce(half(largest, j), part, AX, ALU.max))
                nc.vector.tensor_sub(part, part, over_row(half(largest, j))).then_inc(S["pool_sub"], 1)
            dve.wait_ge(S["setup"], 2)
            for j in range(2):
                part = half(pool_p, j)
                dve.wait_ge(S["pool_exp"], j + 1)
                setup(nc.vector.tensor_reduce(half(total, j), part, AX, ALU.add))
                setup(nc.vector.tensor_mul(half(total, j), half(total, j), half(count[0], j)))
                nc.vector.reciprocal(half(largest, j), half(total, j)).then_inc(S["dve_chain"], 1)
                steps[0] += 1
                dve.wait_ge(S["dve_chain"], steps[0])
                nc.vector.tensor_mul(part, part, over_row(half(largest, j))).then_inc(S["pool_prob"], 1)
                dve.wait_ge(S["pool_prob"], HALF * j + j + 1)
                for i in range(HALF * j, HALF * j + HALF):
                    if i >= 2:
                        dve.wait_ge(S["pooled_ps"], i - 1)
                    for s in range(SPT):
                        rows = slice(SEQ * s, SEQ * s + SEQ)
                        last = nc.vector.transpose(pool_pt[rows, i % 2, :, s, :], pool_p[rows, bass.ts(i, TILES), :])
                    last.then_inc(S["pool_prob"], 1)
            assert steps[0] == CHAIN_BASE, steps[0]

            rotate(0)
            for p in range(UNITS):
                if p == 6:
                    for i in range(2):
                        dve.wait_ge(S[f"h_stored{i}"], 16 * HALF)
                attention_half_step(p, 0)
                attention_step(p, 0)

            def switch(blk):
                dve.wait_ge(S["c_hi_ready"], blk + 1)
                nc.vector.tensor_sub(c_lo[:, :], c2[:, :], c_hi[:, :].bitcast(F32)).then_inc(S["c_lo_ready"], 1)

            switch(0)
            rotate(1)

            def experts(b, following):
                for p in range(UNITS):
                    dve.wait_ge(S["silu_done"], b * UNITS + p + 1)
                    if p < NPAIR:
                        dve.wait_ge(cwb_in[p % NCW], b * (16 * NPAIR // NCW) + 16 * (p // NCW + 1))
                        nc.vector.tensor_mul(act_w[:, p % NH, :], gate_bank(p)[:, :], cwb[:, p % NCW, :])\
                            .then_inc(S["weighted"], 1)
                    if following is not None:
                        attention_half_step(p, following)
                    if p < NPAIR:
                        dve.wait_ge(S["up_done"], b * NPAIR + p + 1)
                        dve.wait_ge(S["weighted"], (b + 1) * NPAIR + p + 1)
                    else:
                        dve.wait_ge(S["down_done"], b * UNITS + p - NH + 1)
                    n, up = (P, up_bank(p)[:, :]) if p < NPAIR else (F, gate_bank(p)[F:2 * F, :])
                    nc.vector.tensor_mul(hid[0:n, p % NH, :], act_w[0:n, p % NH, :], up).then_inc(S["hid_ready"], 1)
                    if following is not None:
                        attention_step(p, following)
                dve.wait_ge(S["hi_ready"], b * UNITS + UNITS)
                nc.vector.tensor_sub(hid_lo[0:F, NPAIR % NH, :], hid[0:F, NPAIR % NH, :],
                                     hid_hi[0:F, NPAIR % NH, :].bitcast(F32)).then_inc(S["shared_lo_ready"], 1)
                if following is not None:
                    switch(following)
                    rotate(following + 1)
                dve.wait_ge(S["down_done"], b * UNITS + UNITS)
                dve.wait_ge(S["y_free"], b * 16 + 16)
                dve.wait_ge(S["x2_moved"], b + 1)
                nc.vector.tensor_add(y[:, :], Y[:, :], x2[:, :]).then_inc(S["y_ready"], 1)
                dve.wait_ge(S["y_ready"], b + 1)
                dve.sem_inc(S["sum_free"], 1)

            with dve.Fori(0, NBLK - 1) as b:
                experts(b, b + 1)
            experts(NBLK - 1, None)

        @block.tensor
        def _(pe):
            def mm(dst, lhsT, rhs, **k):
                k.setdefault("start", True)
                k.setdefault("stop", True)
                return nc.tensor.matmul(dst, lhsT, rhs, **k)

            def first_products(blk):
                if isinstance(blk, int) and blk == 0:
                    pe.wait_ge(S["pooled_ready"], NBLK)
                else:
                    pe.wait_ge(S["h_in"], blk * 16)
                wait(pe, "cwT_ready", blk)
                mm(A0[:, :], rope_w[:, :], h_feat[:, :]).then_inc(S["rope_ps"], 1)
                mm(A1[:, :], k_w[:, :], h_feat[:, :]).then_inc(S["k_ps"], 1)
                mm(A2[:, :], W["q"], h_feat[:, :]).then_inc(S["q_ps"], 1)

            def attention_step(p, blk):
                if p == UNITS - 1:
                    first_products(blk + 1)
                elif p == 2:
                    pe.wait_ge(S["rot_ready"], blk + 1)
                    for t in range(TILES - 1):
                        mm(A0[:, bass.ts(t, P)], h_feat[:, bass.ts(t, P)], v_w[:, :])
                elif p == 5:
                    pe.wait_ge(S["q_ready"], blk * NG + NG)
                    if isinstance(blk, int):
                        pe.wait_ge(S["krope_ready"], 1)
                    else:
                        pe.wait_ge(S["krope_in"], blk * 16)
                    t = TILES - 1
                    last = mm(A0[:, bass.ts(t, P)], h_feat[:, bass.ts(t, P)], v_w[:, :])
                    last.then_inc(S["v_ps"], 1)
                    for s in range(SPB):
                        t, r = divmod(s, SPT)
                        last = mm(A2[32 * r:32 * r + 32, bass.ts(t, SEQ)], rope_sum[0:ROPE, bass.ts(s, SEQ)],
                                  k_rope[:, bass.ts(s, SEQ)])
                    last.then_inc(S["rope_score_ps"], 1)
                elif 6 <= p < 10:
                    t = p - 6
                    if t == 0:
                        pe.wait_ge(S["rope_mask_ready"], blk + 1)
                        pe.wait_ge(S["k_ready"], blk * HG + HG)
                    elif t >= 2:
                        pe.wait_ge(S["biased_tile"], blk * TILES + t - 1)
                    for g in range(NG):
                        for r in range(SPT):
                            tok = bass.ts(t * SPT + r, SEQ)
                            last = mm((A2, A1)[t % 2][32 * r:32 * r + 32, bass.ts(g, P)], q_grp[:, g, tok], k_blk[:, :, tok])
                    last.then_inc(S["score_tile_ps"], 1)
                if 12 <= p < 16:
                    t = p - 12
                    pe.wait_ge(S["prob_tile"], blk * TILES + t + 1)
                    if t == 0:
                        pe.wait_ge(S["biased_tile"], blk * TILES + TILES)
                    else:
                        pe.wait_ge(S["probT_ready"], blk * TILES + t)
                    for g in range(NG):
                        last = nc.tensor.transpose(A1[:, bass.ts(g, P)], s_t[:, t, bass.ts(g, P)], C["ident"])
                    last.then_inc(S["probT_ps"], 1)
                if 13 <= p < 17:
                    t = p - 13
                    pe.wait_ge(S["probT_ready"], blk * TILES + t + 1)
                    if t == 0:
                        if isinstance(blk, int):
                            pe.wait_ge(S["v_ready"], TILES)
                        else:
                            pe.wait_ge(S["weighted"], blk * NPAIR + LENT + 1)
                    elif t == 1 and not isinstance(blk, int):
                        pe.wait_ge(S["hid_ready"], (blk - 1) * UNITS + LENT + 1)
                    elif t >= 2:
                        pe.wait_ge(S["att_ready"], blk * TILES + t - 1)
                    for g in range(NG):
                        for r in range(SPT):
                            last = mm((A0, A2)[t % 2][32 * r:32 * r + 32, bass.ts(g, HG * VC)],
                                      pt_sb[:, t % 2, g * P + 32 * r:g * P + 32 * r + 32], v_blk[:, t, r, g, :])
                    last.then_inc(S["av_ps"], 1)
                elif p == 17:
                    pe.wait_ge(S["att_ready"], blk * TILES + TILES)
                    for t in range(TILES):
                        last = nc.tensor.transpose(A1[:, bass.ts(t, P)], att[:, t, :, :].rearrange("p h d -> p (h d)"),
                                                   C["ident"])
                    last.then_inc(S["attT_ps"], 1)
                elif p == 18:
                    pe.wait_ge(S["attT_ready"], blk + 1)
                    mm(A0[:, :], W["o"], att_feat[:, :]).then_inc(S["wo_ps"], 1)
                elif p == 19:
                    pe.wait_ge(S["x2_ready"], blk + 1)
                    pe.wait_ge(S["wcat_in"], blk * (16 * SPB) + 16 * SPB)
                    for s in range(SPB):
                        t, r = divmod(s, SPT)
                        last = mm(A1[32 * r:32 * r + 32, bass.ts(t, D)], x2_next[:, bass.ts(s, SEQ)], wcat[:, s, :])
                    last.then_inc(S["c2tok_ps"], 1)
                elif p == 20:
                    pe.wait_ge(S["c2tok_ready"], blk + 1)
                    for t in range(TILES):
                        last = nc.tensor.transpose(A0[:, bass.ts(t, P)], c2_tok[:, bass.ts(t, D)], C["ident"])
                    last.then_inc(S["c2_ps"], 1)
                elif p == 21:
                    pe.wait_ge(S["c2_ready"], blk + 1)
                    for t in range(TILES):
                        last = mm(A2[:, bass.ts(t, E)], c2[:, bass.ts(t, P)], W["gate"])
                    last.then_inc(S["gate_ps"], 1)
                elif p == CWT:
                    pe.wait_ge(S["cw_ready"], blk + 1)
                    for t in range(0, TILES, 2):
                        last = nc.tensor.transpose(A0[:, bass.ts(t // 2, P)], cw[:, t:t + 2, :].rearrange("p t e -> p (t e)"),
                                                   C["ident"])
                    last.then_inc(S["cwT_ps"], 1)

            pe.wait_ge(S["consts_in"], CONSTS)
            first, width = W_COLS["k"][0], 2 * D + 2 * ROPE
            mm(A2[:, 0:width], W["kvT"], w[:, first:first + width]).then_inc(S["fold_ps"], 1)

            def warm(n):
                for _ in range(n):
                    mm(Y[:, 0:P], C["ident"], C["ident"])

            def pool_hidden(j):
                pe.wait_ge(S[f"xf_in{j}"], 16 * HALF)
                for i in range(HALF):
                    for t in range(TILES):
                        last = mm(G[j][32 * t:32 * t + 32, bass.ts(i, P)], W["w1"], xf_in[HALF * j + i][:, bass.ts(t, P)])
                last.then_inc(S["hidden_ps"], 1)

            def pool_scores(j):
                pe.wait_ge(S["tanh_done"], j + 1)
                dst = U[j][:, :].rearrange("p (i t l) -> p i t l", t=TILES, l=SEQ)
                for t in range(TILES):
                    for s in range(SPT):
                        last = mm(dst[32 * s:32 * s + 32, :, t, :], vrep[:, t, :],
                                  hidden[:, HALF * j:HALF * j + HALF, bass.ts(s, SEQ)])
                last.then_inc(S["score_ps"], 1)

            def turn(i):
                if i >= 2:
                    pe.wait_ge(S["xt_ready"], i - 1)
                for t in range(TILES):
                    last = nc.tensor.transpose((A0, A1)[i % 2][:, bass.ts(t, P)], xf_in[i][:, bass.ts(t, P)], C["ident"])
                last.then_inc(S["xt_ps"], 1)

            warm(WARM_LOADS)
            pool_hidden(0)
            for i in range(HALF):
                turn(i)
            pool_hidden(1)
            pe.wait_ge(S["dve_chain"], CHAIN_SETUP)
            pool_scores(0)
            for i in range(HALF, HALF + 2):
                turn(i)
            pool_scores(1)
            for i in range(HALF + 2, NBLK):
                turn(i)
            warm(WARM_SOFTMAX)
            mm(Y[:, 0:NSEQ], cat_table, onehot).then_inc(S["cat_ps"], 1)
            pe.wait_ge(S["xt_ready"], NBLK)
            for i in range(NBLK):
                pe.wait_ge(S["pool_prob"], i // HALF + i + 2)
                if i >= 2:
                    pe.wait_ge(S["pooled_ready"], i - 1)
                for t in range(TILES):
                    last = mm((A0, A1)[i % 2][:, bass.ts(t, P)], xt_in[i][:, bass.ts(t, D)],
                              pool_pt[:, i % 2, t, :, :].rearrange("p s j -> p (s j)"))
                last.then_inc(S["pooled_ps"], 1)
            pe.wait_ge(S["folded"], 1)
            pe.wait_ge(S["cat_read"], 1)
            pe.wait_ge(S["setup"], 2)
            warm(WARM_POOLED)
            first_products(0)
            for p in range(UNITS):
                attention_step(p, 0)
                warm(WARM.get(p, 0))
            pe.wait_ge(S["split_lo"], LATER)

            def three(dst, w_hi, w_lo, m_hi, m_lo, first, final):
                mm(dst, w_hi, m_hi, start=first, stop=False)
                mm(dst, w_lo, m_hi, start=False, stop=False)
                return mm(dst, w_hi, m_lo, start=False, stop=final)

            def experts(b, following):
                pe.wait_ge(S["c_lo_ready"], b + 1)

                def down(p):
                    n = P if p < NPAIR else F
                    if p < NPAIR:
                        pe.wait_ge(S["lo_ready"], b * NPAIR + p + 1)
                    else:
                        pe.wait_ge(S["shared_lo_ready"], b + 1)
                    if p == 0:
                        pe.wait_ge(S["split_lo"], NSPLIT + 1)
                        pe.wait_ge(S["sum_free"], b + 1)
                    three(Y[:, :], wd_hi[0:n, p, :], wd_lo[0:n, p, :], hid_hi[0:n, p % NH, :], hid_lo[0:n, p % NH, :],
                          p == 0, p == UNITS - 1).then_inc(S["down_done"], 1)

                for p in range(UNITS):
                    if p == LENT:
                        if following is not None:
                            pe.wait_ge(S["v_ready"], following * TILES + TILES)
                    elif p >= 2:
                        pe.wait_ge(S["weighted"], (b + 1) * NPAIR + (p - 3 if p == LENT + 2 else p - 1))
                    three(gate_bank(p)[:, :], wg_hi[:, p, :], wg_lo[:, p, :], c_hi[:, :], c_lo[:, :], True, True)\
                        .then_inc(S["gate_done"], 1)
                    if p >= NH:
                        down(p - NH)
                    if p < NPAIR:
                        if p == LENT:
                            if following is not None:
                                pe.wait_ge(S["biased_tile"], following * TILES + TILES)
                        elif p >= 2:
                            pe.wait_ge(S["hid_ready"], b * UNITS + (p - 3 if p == LENT + 2 else p - 1))
                        three(up_bank(p)[:, :], wu_hi[:, p, :], wu_lo[:, p, :], c_hi[:, :], c_lo[:, :], True, True)\
                            .then_inc(S["up_done"], 1)
                    if following is not None:
                        attention_step(p, following)
                for p in range(UNITS - NH, UNITS):
                    down(p)

            pe.sem_inc(S["sum_free"], 1)
            with pe.Fori(0, NBLK - 1) as b:
                experts(b, b + 1)
            experts(NBLK - 1, None)


def kernel(x, itok_B_0_2, itok_B_0_63, L0_cond_W1, L0_cond_b1, L0_cond_v, L0_attn_W_kv_down, L0_attn_W_k_up,
           L0_attn_W_v_up, L0_attn_W_q, L0_attn_W_q_rope, L0_attn_W_k_rope, L0_attn_W_o, L0_cond2_W, L0_cond2_b,
           L0_ffn_gate_w, L0_ffn_gate_bias, L0_ffn_We_gate, L0_ffn_We_up, L0_ffn_We_down, L0_ffn_Ws_gate,
           L0_ffn_Ws_up, L0_ffn_Ws_down):
    import concourse.bacc as bacc
    from concourse.bass_utils import run_bass_kernel_spmd

    def swapped(a):
        a = np.asarray(a)
        return np.concatenate([a, a[:, ROPE // 2:], a[:, :ROPE // 2]], 1)

    def experts_in(a):
        return np.ascontiguousarray(np.transpose(np.asarray(a), (1, 0, 2)).reshape(D, E * F))

    tokens = np.asarray(x).reshape(NSEQ * SEQ, D)
    arrays = {
        "x_tok": tokens.reshape(NBLK * TILES, P, D).transpose(1, 0, 2),
        "x_feat": tokens.T,
        "prompt": np.repeat(np.asarray(itok_B_0_2).reshape(NSEQ // SPT, SPT).T, SEQ, axis=0),
        "cats": np.asarray(itok_B_0_63).reshape(1, NSEQ),
        "cond_w": np.asarray(L0_cond2_W).reshape(CATS * D, D),
        "cond_b": np.asarray(L0_cond2_b),
        "weights": np.concatenate([np.asarray(a) for a in (
            np.asarray(L0_attn_W_kv_down).T, L0_attn_W_q, L0_attn_W_k_up, L0_attn_W_v_up, swapped(L0_attn_W_k_rope),
            L0_attn_W_o, swapped(L0_attn_W_q_rope), L0_cond_W1, np.tile(np.asarray(L0_cond_b1), TILES)[:, None],
            np.tile(np.asarray(L0_cond_v), TILES)[:, None], np.asarray(L0_ffn_gate_w).T)], 1),
        "consts": shape_constants(),
        "gate_bias": np.asarray(L0_ffn_gate_bias).reshape(1, E),
        "we_gate": experts_in(L0_ffn_We_gate),
        "we_up": experts_in(L0_ffn_We_up),
        "we_down": np.asarray(L0_ffn_We_down).reshape(NPAIR, 2 * F, D).transpose(1, 0, 2).reshape(2 * F, NPAIR * D),
        "ws_gu": np.concatenate([np.asarray(L0_ffn_Ws_gate), np.asarray(L0_ffn_Ws_up)], 1),
        "ws_down": np.asarray(L0_ffn_Ws_down),
    }
    nc = bacc.Bacc("TRN2", target_bir_lowering=False, num_devices=1)
    feeds, args = {}, []
    for name, a in arrays.items():
        a = np.ascontiguousarray(a)
        feeds[f"in_{name}"] = a
        args.append(nc.dram_tensor(f"in_{name}", a.shape, mybir.dt.from_np(a.dtype), kind="ExternalInput").ap())
    result = nc.dram_tensor("out_feat", (D, NSEQ * SEQ), F32, kind="ExternalOutput").ap()
    adaln_attention_moe(nc, *args, result)
    got = run_bass_kernel_spmd(nc, [feeds], core_ids=[0]).results[0]["out_feat"]
    return np.ascontiguousarray(got.T.reshape(NSEQ, SEQ, D))
```
